# Optimizing a Trainium2 kernel written in Bass

```python
import numpy as np
import jax
import jax.numpy as jnp

def _softmax(x, axis=-1):
    return jax.nn.softmax(x, axis=axis)

def _gelu(x):
    return jax.nn.gelu(x, approximate=True)

def _silu(x):
    return jax.nn.silu(x)

def _sigmoid(x):
    return jax.nn.sigmoid(x)

def _layernorm(x, axis=-1, eps=1e-05):
    m = jnp.mean(x, axis=axis, keepdims=True)
    v = jnp.var(x, axis=axis, keepdims=True)
    return (x - m) / jnp.sqrt(v + eps)

def _scatter_add(tgt, idx, src, axis=0):
    return tgt.at[idx].add(src)

def _segment_sum(src, seg, n):
    return jax.ops.segment_sum(src, seg, n)
kernel_name = 'mk_adj_preln_d2_adj_r2_d8d229'

def setup_inputs(seed: int=0):
    np.random.seed(seed)
    _w = jnp.asarray

    def _rec_inputs():
        import jax
        import jax.numpy as jnp
        _gk = jax.random.key(seed)
        x = -0.0002928 + 1 * jax.random.normal(jax.random.fold_in(_gk, 1), (3327, 256), jnp.float32)
        _a = jax.random.bernoulli(jax.random.fold_in(_gk, 2), 0.00120228, (3327, 3327))
        _a = jnp.logical_or(_a, jnp.eye(3327, dtype=bool))
        _af = _a.astype(jnp.float32)
        adj = _af
        return (x, adj)
    x, adj = _rec_inputs()

    def _L0_gnn_setup():
        import jax, jax.numpy as jnp
        import numpy as np
        N = 4096
        F_IN = 256
        F_OUT = 256
        DENSITY = 0.01
        key = jax.random.key(seed)
        k_x, k_adj, k_w, k_b = jax.random.split(key, 4)
        input_features = jax.random.normal(k_x, (N, F_IN), dtype=jnp.float32)
        adj = (jax.random.uniform(k_adj, (N, N)) < DENSITY).astype(jnp.float32)
        idx = jnp.arange(N)
        adj = adj.at[idx, idx].set(1.0)
        W = jax.random.normal(k_w, (F_IN, F_OUT), dtype=jnp.float32) / np.sqrt(F_IN)
        b = jax.random.normal(k_b, (F_OUT,), dtype=jnp.float32) * 0.01
        return {'input_features': input_features, 'adj': adj, 'W': W, 'b': b}
    _L0_gnn_all = _L0_gnn_setup()
    _L0_gnn_in = {k: v for k, v in _L0_gnn_all.items() if k in ('W', 'b')}
    del _L0_gnn_all

    def _L1_gnn_setup():
        import jax, jax.numpy as jnp
        import numpy as np
        N, D_IN, D_ATTN, STEPS, P_NUC, TAU = (2048, 256, 64, 2, 0.9, 1.0)
        LN_EPS = 1e-05

        def _xavier(key, shape):
            fan_in, fan_out = (shape[-2], shape[-1])
            lim = np.sqrt(6.0 / (fan_in + fan_out))
            return jax.random.uniform(key, shape, jnp.float32, -lim, lim)

        def _adj_from_feats(Xa, W1, W2, W3):
            Q = Xa @ W1
            K = Xa @ W3
            logits = Q @ W2 @ K.T / TAU
            idx = jnp.argsort(-logits, axis=1)
            vals = jnp.take_along_axis(logits, idx, axis=1)
            csum = jnp.cumsum(jax.nn.softmax(vals, axis=1), axis=1)
            k_i = jnp.sum(csum < P_NUC, axis=1) + 1
            ranks = jnp.arange(logits.shape[1])[None, :]
            keep_sorted = ranks < k_i[:, None]
            inv = jnp.argsort(idx, axis=1)
            keep = jnp.take_along_axis(keep_sorted, inv, axis=1)
            masked = jnp.where(keep, logits, -jnp.inf)
            return jax.nn.softmax(masked, axis=1)
        key = jax.random.key(seed)
        ks = jax.random.split(key, 9)
        return {'X': jax.random.normal(ks[0], (N, D_IN), jnp.float32), 'S': jax.random.uniform(ks[1], (N, N), jnp.float32), 'W1': _xavier(ks[2], (D_IN, D_ATTN)), 'W2': _xavier(ks[3], (D_ATTN, D_ATTN)), 'W3': _xavier(ks[4], (D_IN, D_ATTN)), 'U1': _xavier(ks[5], (STEPS, D_IN, D_IN)), 'U2': _xavier(ks[6], (STEPS, D_IN, D_IN)), 'U3': _xavier(ks[7], (STEPS, D_IN, D_IN)), 'gamma': jnp.ones((D_IN,), jnp.float32), 'beta': jnp.zeros((D_IN,), jnp.float32)}
    _L1_gnn_all = _L1_gnn_setup()
    _L1_gnn_in = {k: v for k, v in _L1_gnn_all.items() if k in ('W1', 'W2', 'W3', 'U1', 'U2', 'U3', 'gamma', 'beta')}
    del _L1_gnn_all
    return {'x': x, 'adj': adj, 'L0_gnn_W': _L0_gnn_in['W'], 'L0_gnn_b': _L0_gnn_in['b'], 'L1_gnn_W1': _L1_gnn_in['W1'], 'L1_gnn_W2': _L1_gnn_in['W2'], 'L1_gnn_W3': _L1_gnn_in['W3'], 'L1_gnn_U1': _L1_gnn_in['U1'], 'L1_gnn_U2': _L1_gnn_in['U2'], 'L1_gnn_U3': _L1_gnn_in['U3'], 'L1_gnn_gamma': _L1_gnn_in['gamma'], 'L1_gnn_beta': _L1_gnn_in['beta']}

def reference(x, adj, L0_gnn_W, L0_gnn_b, L1_gnn_W1, L1_gnn_W2, L1_gnn_W3, L1_gnn_U1, L1_gnn_U2, L1_gnn_U3, L1_gnn_gamma, L1_gnn_beta):
    import jax
    import jax.numpy as jnp

    def _L0_gnn_ref(input_features, adj, W, b):
        import jax, jax.numpy as jnp
        import numpy as np
        N = 4096
        F_IN = 256
        F_OUT = 256
        DENSITY = 0.01
        A = (adj != 0).astype(input_features.dtype)
        hidden = input_features @ W + b
        deg = jnp.sum(A, axis=0)
        return A @ hidden / deg[:, None]

    def _L1_gnn_ref(X, S, W1, W2, W3, U1, U2, U3, gamma, beta):
        import jax, jax.numpy as jnp
        import numpy as np
        N, D_IN, D_ATTN, STEPS, P_NUC, TAU = (2048, 256, 64, 2, 0.9, 1.0)
        LN_EPS = 1e-05

        def _xavier(key, shape):
            fan_in, fan_out = (shape[-2], shape[-1])
            lim = np.sqrt(6.0 / (fan_in + fan_out))
            return jax.random.uniform(key, shape, jnp.float32, -lim, lim)

        def _adj_from_feats(Xa, W1, W2, W3):
            Q = Xa @ W1
            K = Xa @ W3
            logits = Q @ W2 @ K.T / TAU
            idx = jnp.argsort(-logits, axis=1)
            vals = jnp.take_along_axis(logits, idx, axis=1)
            csum = jnp.cumsum(jax.nn.softmax(vals, axis=1), axis=1)
            k_i = jnp.sum(csum < P_NUC, axis=1) + 1
            ranks = jnp.arange(logits.shape[1])[None, :]
            keep_sorted = ranks < k_i[:, None]
            inv = jnp.argsort(idx, axis=1)
            keep = jnp.take_along_axis(keep_sorted, inv, axis=1)
            masked = jnp.where(keep, logits, -jnp.inf)
            return jax.nn.softmax(masked, axis=1)
        n = X.shape[0]
        S = S + jnp.eye(n, dtype=X.dtype)
        Rf = S / jnp.clip(S.sum(axis=1, keepdims=True), 1e-12)
        Rb = S / jnp.clip(S.sum(axis=0), 1e-12)[:, None]
        Xf, Xb, Xa = (X, X, X)
        Z = jnp.zeros_like(X)
        for s in range(STEPS):
            A = _adj_from_feats(Xa, W1, W2, W3)
            Xf = Rf @ Xf
            Xb = Rb @ Xb
            Xa = A @ Xa
            Z = Z + (Xf @ U1[s] + Xb @ U2[s] + Xa @ U3[s])
        Y = X + Z
        mu = Y.mean(axis=-1, keepdims=True)
        var = Y.var(axis=-1, keepdims=True)
        return (Y - mu) / jnp.sqrt(var + LN_EPS) * gamma + beta
    h = jnp.maximum(_layernorm(x, axis=-1), 0.0)
    x = x + _L0_gnn_ref(h, adj, L0_gnn_W, L0_gnn_b)
    h = jnp.maximum(_layernorm(x, axis=-1), 0.0)
    x = x + _L1_gnn_ref(h, adj, L1_gnn_W1, L1_gnn_W2, L1_gnn_W3, L1_gnn_U1, L1_gnn_U2, L1_gnn_U3, L1_gnn_gamma, L1_gnn_beta)
    return x

_drawn_inputs = setup_inputs


def setup_inputs(seed=0):
    import zlib

    import numpy as np

    out = dict(_drawn_inputs(seed))
    spreads = {'L1_gnn_gamma': (1.0, 0.2), 'L1_gnn_beta': (0.0, 0.1)}
    factors = {'L0_gnn_b': 4.508}
    for name, (base, spread) in spreads.items():
        noise = np.random.default_rng([zlib.crc32(name.encode()), seed]).standard_normal(out[name].shape)
        drawn = base * np.exp(spread * noise) if base else spread * noise
        out[name] = jnp.asarray(drawn.astype(out[name].dtype))
    for name, factor in factors.items():
        out[name] = (out[name] * factor).astype(out[name].dtype)
    return out
```

```python
import math

import numpy as np
import concourse.bass as bass
from concourse import mybir


class Idx:

    def __init__(self, g, off, base=0):
        self.g, self.off, self.base = g, off, base
        self.static = isinstance(g, int)
        self.t = 2 * g + off
        self.n = 2 * g + (off + base)
        self.slot = off % 2
        self.use = g + (off + base) // 2
        self.use_here = g + off // 2

    def __add__(self, d):
        return Idx(self.g, self.off + d, self.base)

    def inside(self, tiles):
        return not self.static or 0 <= self.t < tiles

    def ring(self, per, c):
        s = per * (self.off + self.base) + c
        return s % 2, per * self.g + s // 2


def gnn_program(nc, x, adj, W, b, W1, W2, W3, U1, U2, U3, gamma, beta, out):
    f32, f16, bf16 = mybir.dt.float32, mybir.dt.float16, mybir.dt.bfloat16
    ALU, ACT, AX = mybir.AluOpType, mybir.ActivationFunctionType, mybir.AxisListType

    P = 128
    N, D = x.shape
    DA = W2.shape[0]
    KD = D // P
    T = -(-N // P)
    NP = T * P
    LAST = N - (T - 1) * P
    EPS = 1e-5
    SCALE = 1024.0
    NUCLEUS = 0.9
    CW = 512
    LCH = [(c, min(CW, N - c)) for c in range(0, N, CW)]
    TCH = [(c, min(4, T - c)) for c in range(0, T, 4)]
    HCH = [(c, min(8, T - c)) for c in range(0, T, 8)]
    NL, NT, NH = len(LCH), len(TCH), len(HCH)
    RANGE = math.log(N / (1 - NUCLEUS)) + 0.01
    EVALS = 24

    adjT_d = nc.dram_tensor("adjT_d", [T, P, T * P], f16, kind="Internal").ap()
    x1_d = nc.dram_tensor("x1_d", [P, T * D], f32, kind="Internal").ap()
    y_d = nc.dram_tensor("y_d", [T, P, D], f32, kind="Internal").ap()
    xa_d = nc.dram_tensor("xa_d", [T, P, D], f32, kind="Internal").ap()

    def sb(name, shape, dt):
        return nc.alloc_sbuf_tensor(name, shape, dt)

    sem_names = {}

    def sem(name):
        if name not in sem_names:
            sem_names[name] = nc.alloc_semaphore(name)
        return sem_names[name]

    def sem2(name):
        return [sem(f"{name}_{u}") for u in range(2)]

    regA = sb("regA", [P, T * D], f32)
    regB = sb("regB", [P, T * 2 * D], f32)
    xa = sb("xa", [P, T, D], f32)
    keys = sb("keys", [P, NP], f32)
    queries = sb("queries", [P, NP], f32)
    at = [sb(f"at{u}", [P, T, P], f16) for u in range(2)]
    pb_all = sb("pb_all", [P, 2 * NP], f32)
    pb = [pb_all[:, u * NP:(u + 1) * NP] for u in range(2)]
    junk = sb("junk", [P, NP], bf16)
    pt = [sb(f"pt{u}", [P, CW], f32) for u in range(2)]
    parts = regA[:, :].bitcast(f16).rearrange("p (t c) -> p t c", c=2 * D)
    yall = regA[:, :].rearrange("p (t d) -> p t d", d=D)
    parts_fb = regB[:, :].bitcast(f16).rearrange("p (t c) -> p t c", c=4 * D)
    adj_in = [regB[:, u * NP:(u + 1) * NP] for u in range(2)]
    adj16 = [regB[:, (2 * NP + u * NP // 2):(2 * NP + (u + 1) * NP // 2)].bitcast(f16) for u in range(2)]
    x_all = pb_all[:, :].rearrange("p (t d) -> p t d", d=D)

    ident = sb("ident", [P, P], f32)
    ident16 = sb("ident16", [P, P], f16)
    padone = sb("padone", [P, 1], f32)
    early = junk[:, :].bitcast(f32)
    w_sb = early[:, 0:KD * D].rearrange("p (k d) -> p k d", d=D)
    b_bc = early[:, KD * D:(KD + 1) * D]
    e0 = (KD + 1) * D
    w1_sb = early[:, e0:e0 + KD * DA].rearrange("p (k d) -> p k d", d=DA)
    w1t_sb = early[0:DA, e0 + KD * DA:e0 + KD * (DA + P)].rearrange("p (k d) -> p k d", d=P)
    w2_sb = early[0:DA, e0 + KD * (DA + P):e0 + KD * (DA + P) + DA]
    gamma_bc = keys[:, 0:D]
    beta_bc = keys[:, D:2 * D]
    wq_sb = sb("wq_sb", [P, KD, DA], f32)
    w3_sb = sb("w3_sb", [P, KD, DA], f32)
    u_sb = sb("u_sb", [P, 3, KD, D], f32)
    stats = sb("stats", [P, T, 6], f32)
    mv = sb("mv", [P, T, 2], f32)
    ve = sb("ve", [P, T], f32)
    sd = sb("sd", [P, T], f32)
    lt = sb("lt", [P, T], f32)
    ly = sb("ly", [P, T, 1], f32)
    lb = sb("lb", [P, T, 1], f32)
    rowsum = sb("rowsum", [P, T, 1], f32)
    colsum = sb("colsum", [P, T], f32)
    cs_tmp = sb("cs_tmp", [P, T], f32)
    rdeg = sb("rdeg", [P, T, 1], f32)
    rinv = sb("rinv", [P, T, 1], f32)
    cinv = sb("cinv", [P, T, 1], f32)
    cinv_r = sb("cinv_r", [P, T, 1], f32)
    rinv_s = sb("rinv_s", [P, T, 1], f32)
    ratio = sb("ratio", [P, 1], f32)
    ratio_all = sb("ratio_all", [P, 1], f32)
    kappa = sb("kappa", [P, 1], f32)
    t256 = [sb(f"t256_{u}", [P, 2, D], f32) for u in range(2)]
    xf_sb = [sb(f"xf_sb{u}", [P, D], f32) for u in range(2)]
    xb_sb = [sb(f"xb_sb{u}", [P, D], f32) for u in range(2)]
    xo_sb = [sb(f"xo_sb{u}", [P, D], f32) for u in range(2)]
    xk_sb = sb("xk_sb", [P, D], f32)
    zt = sb("zt", [P, 6, P], f32)
    y_sb = [sb(f"y_sb{u}", [P, D], f32) for u in range(2)]
    qs = [sb(f"qs{u}", [P, P], f32) for u in range(2)]
    negmax = [sb(f"negmax{u}", [P, 1], f32) for u in range(2)]
    zsum = [sb(f"zsum{u}", [P, 1], f32) for u in range(2)]
    target = sb("target", [P, 1], f32)
    thr = sb("thr", [P, 1], f32)
    mass = sb("mass", [P, 1], f32)
    step_up = sb("step_up", [P, 1], f32)
    kept = sb("kept", [P, 1], f32)
    rkept = [sb(f"rkept{u}", [P, 1], f32) for u in range(2)]

    bank = [nc.alloc_psum_tensor(f"bank{i}", [P, CW], f32) for i in range(8)]

    def bank16(i):
        return bank[i][:, :].bitcast(f16)

    class Chain:

        def __init__(self, eng, name, base=0):
            self.eng, self.sem, self.base, self.count = eng, sem(name), base, 0

        def link(self, ins):
            self.count += 1
            ins.then_inc(self.sem, 1)
            self.eng.wait_ge(self.sem, self.base + self.count)

    def layernorm_scalars(dve, call, scale):
        ch = Chain(dve, "ln_chain", base=7 * call)
        ch.link(nc.vector.tensor_scalar(ve[:, :], mv[:, :, 1], EPS, None, ALU.add))
        ch.eng.sem_inc(sem("ln_var"), 1)
        dve.wait_ge(sem("ln_sqrt"), call + 1)
        ch.link(nc.vector.reciprocal(sd[:, :], sd[:, :]))
        ch.link(nc.vector.tensor_tensor(lt[:, :], sd[:, :], sd[:, :], ALU.mult))
        ch.link(nc.vector.tensor_tensor(lt[:, :], lt[:, :], ve[:, :], ALU.mult))
        ch.link(nc.vector.tensor_scalar(lt[:, :], lt[:, :], -0.5 * scale, 1.5 * scale, ALU.mult, ALU.add))
        ch.link(nc.vector.tensor_tensor(ly[:, :, 0], sd[:, :], lt[:, :], ALU.mult))
        ch.link(nc.vector.tensor_tensor(lt[:, :], mv[:, :, 0], ly[:, :, 0], ALU.mult))
        nc.vector.tensor_scalar(lb[:, :, 0], lt[:, :], -1.0, None, ALU.mult).then_inc(sem("ln_ready"), 1)

    def layernorm_sqrt(act, call):
        act.wait_ge(sem("ln_var"), call + 1)
        nc.scalar.activation(sd[:, :], ve[:, :], ACT.Sqrt).then_inc(sem("ln_sqrt"), 1)

    def sweep(eng, first, loop_from, pairs, last, body, base=0):
        for i in range(first, loop_from):
            body(Idx(0, i, base))
        with eng.Fori(0, pairs) as g:
            for u in range(2):
                body(Idx(g, loop_from + u, base))
        for i in range(loop_from + 2 * pairs, last):
            body(Idx(0, i, base))

    def dyn(i):
        return i.t

    def adj_sweep(eng, body):
        sweep(eng, -2, 3, (T - 6) // 2, T + 1, body)

    def bc(v):
        return v.partition_broadcast(P)

    XH = T // 2
    with nc.Block() as block:

        @block.sync
        def _(sp):
            sp.wait_ge(sem("x_pad_clear"), 1)
            sp.dma_start(x_all[:, 0:XH, :], x[0:XH * P, :].rearrange("(t p) d -> p t d", p=P)).then_inc(sem("x_loaded"), 16)
            sp.dma_start(x_all[:, XH:T - 1, :], x[XH * P:(T - 1) * P, :].rearrange("(t p) d -> p t d", p=P)).then_inc(sem("x_loaded"), 16)
            even = LAST - LAST % 16
            for r0, r1 in ((0, even), (even, LAST)):
                if r1 > r0:
                    sp.dma_start(x_all[r0:r1, T - 1, :], x[(T - 1) * P + r0:(T - 1) * P + r1, :]).then_inc(sem("x_loaded"), 16)
            sp.dma_start(w_sb[:, :, :], W.rearrange("(k p) n -> p k n", p=P)).then_inc(sem("w_loaded"), 16)
            sp.dma_start(b_bc, bc(b)).then_inc(sem("w_loaded"), 16)
            sp.dma_start(w1_sb[:, :, :], W1.rearrange("(k p) n -> p k n", p=P)).then_inc(sem("w_loaded"), 16)
            sp.dma_start(w3_sb[:, :, :], W3.rearrange("(k p) n -> p k n", p=P)).then_inc(sem("w_loaded"), 16)
            sp.dma_start(w2_sb, W2).then_inc(sem("w_loaded"), 16)

            def body(i):
                j = i + 2
                if j.inside(T):
                    sp.wait_ge(sem2("adj_in_free")[j.slot], j.use)
                    if j.static and j.t == T - 1:
                        for r0, r1 in ((0, even), (even, LAST)):
                            if r1 > r0:
                                sp.dma_start(adj_in[j.slot][r0:r1, 0:N], adj[(T - 1) * P + r0:(T - 1) * P + r1, :])\
                                    .then_inc(sem("adj_last_loaded"), 16)
                    else:
                        sp.dma_start(adj_in[j.slot][:, 0:N], adj_t[dyn(j)]).then_inc(sem2("adj_loaded")[j.slot], 16)
                if i.inside(T):
                    sp.wait_ge(sem2("at_ready")[i.slot], NH * (i.use + 1))
                    sp.dma_start(adjT_d[dyn(i)], at[i.slot][:, :, :].rearrange("p t c -> p (t c)"))\
                        .then_inc(sem2("at_stored")[i.slot], 16)

            adj_t = adj[0:(T - 1) * P, :].rearrange("(t p) n -> t p n", p=P)
            adj_sweep(sp, body)
            for u in range(2):
                sp.wait_ge(sem2("at_stored")[u], 16 * (T // 2))

        @block.gpsimd
        def _(pool):
            nc.gpsimd.memset(ident[:, :], 0.0).then_inc(sem("const_chain"), 1)
            nc.gpsimd.memset(padone[:, :], 1.0).then_inc(sem("const_chain"), 1)
            for u in range(2):
                nc.gpsimd.memset(adj_in[u][:, N:NP], 0.0).then_inc(sem("adj_pad"), 1)
            pool.wait_ge(sem("const_chain"), 2)
            nc.gpsimd.affine_select(out=ident[:, :], in_=ident[:, :], compare_op=ALU.not_equal, fill=1.0, base=0,
                                    pattern=[[-1, P]], channel_multiplier=1).then_inc(sem("const_chain"), 1)
            nc.gpsimd.affine_select(out=padone[:, :], in_=padone[:, :], compare_op=ALU.is_ge, fill=0.0, base=-LAST,
                                    pattern=[[0, 1]], channel_multiplier=1).then_inc(sem("consts"), 1)
            pool.wait_ge(sem("const_chain"), 3)
            nc.gpsimd.tensor_copy(ident16[:, :], ident[:, :]).then_inc(sem("consts"), 1)

            def low(i):
                pool.wait_ge(sem2("h_hi")[i.slot], i.use + 1)
                nc.gpsimd.tensor_tensor(parts[:, i.t, D:2 * D], xo_sb[i.slot][:, :], parts[:, i.t, 0:D], ALU.subtract)\
                    .then_inc(sem2("h_lo")[i.slot], 1)
            sweep(pool, 0, 2, T // 2 - 1, T, low)

        @block.scalar
        def _(act):
            layernorm_sqrt(act, 0)
            act.wait_ge(sem("ln_ready"), 1)

            def split(i):
                act.wait_ge(sem2("h_lo")[i.slot], i.use)
                nc.scalar.activation(xo_sb[i.slot][:, :], x_all[:, i.t, :], ACT.Relu, bias=lb[:, i.t, :], scale=ly[:, i.t, :])\
                    .then_inc(sem2("h32")[i.slot], 1)
                act.wait_ge(sem2("h32")[i.slot], i.use + 1)
                nc.scalar.activation(parts[:, i.t, 0:D], xo_sb[i.slot][:, :], ACT.Copy).then_inc(sem2("h_hi")[i.slot], 1)
            sweep(act, 0, 2, T // 2 - 1, T, split)
            act.wait_ge(sem("w1t_psum"), 1)
            nc.scalar.activation(w1t_sb[:, :, :].rearrange("p k c -> p (k c)"), bank[4][0:DA, 0:KD * P], ACT.Copy).then_inc(sem("w1t"), 1)
            act.wait_ge(sem("wq_psum"), 1)
            nc.scalar.activation(wq_sb[:, :, :].rearrange("p k c -> p (k c)"), bank[5][:, 0:KD * DA], ACT.Copy).then_inc(sem("wq"), 1)
            act.wait_ge(sem("adj_pad"), 2)

            def body(i):
                j = i + 2
                if j.inside(T):
                    if j.static and j.t == T - 1:
                        act.wait_ge(sem("adj_last_loaded"), 16 * (2 if LAST % 16 and LAST > 16 else 1))
                    else:
                        act.wait_ge(sem2("adj_loaded")[j.slot], 16 * (j.use + 1))
                    act.wait_ge(sem2("adj16_free")[j.slot], j.use)
                    nc.scalar.activation(adj16[j.slot], adj_in[j.slot], ACT.Copy, accum_out=rowsum[:, j.t, :])\
                        .then_inc(sem2("adj16_ready")[j.slot], 1)
                    act.wait_ge(sem2("adj16_ready")[j.slot], j.use + 1)
                    act.sem_inc(sem2("adj_in_free")[j.slot], 1)
                k = i + -1
                if k.inside(T):
                    act.wait_ge(sem("aggT_psum"), k.n + 1)
                    nc.scalar.activation(zt[:, 0:KD, :], bank[4][:, 0:KD * P].rearrange("p (k c) -> p k c", c=P), ACT.Copy,
                                         scale=1.0 / SCALE).then_inc(sem("aggT"), 1)
                if i.inside(T):
                    act.wait_ge(sem2("agg_psum")[i.slot], i.use + 1)
                    act.wait_ge(sem2("agg_sum")[i.slot], i.use)
                    nc.scalar.activation(t256[i.slot][:, 0, :], bank[2 + i.slot][:, D:2 * D], ACT.Copy)\
                        .then_inc(sem2("agg_lo")[i.slot], 1)
            adj_sweep(act, body)

        @block.vector
        def _(dve):
            ch = Chain(dve, "x_stats_chain")
            half = LAST - LAST % 32
            nc.vector.memset(x_all[half:P, T - 1, :], 0.0).then_inc(sem("x_pad_clear"), 1)
            nc.vector.memset(colsum[:, :], 0.0).then_inc(sem("colsum"), 1)
            dve.wait_ge(sem("x_loaded"), 16 * (3 + (1 if LAST % 16 and LAST > 16 else 0)))
            with dve.Fori(0, T) as t:
                nc.vector.bn_stats(stats[:, t, :], x_all[:, t, :]).then_inc(sem("ln_stats"), 1)
            dve.wait_ge(sem("ln_stats"), 1 * T)
            for t in range(T):
                nc.vector.bn_aggr(mv[:, t, :], stats[:, t, :]).then_inc(sem("ln_mv"), 1)
            dve.wait_ge(sem("ln_mv"), 1 * T)
            layernorm_scalars(dve, 0, SCALE)
            dve.wait_ge(sem("w_loaded"), 16 * 5)

            def body(i):
                j = i + 1
                if j.inside(T):
                    dve.wait_ge(sem2("at_used")[j.slot], j.use)
                    dve.wait_ge(sem2("at_stored")[j.slot], 16 * j.use)
                    for c, (t0, n) in enumerate(HCH):
                        s, use = j.ring(NH, c)
                        dve.wait_ge(sem2("tr_psum")[s], use + 1)
                        nc.vector.tensor_copy(at[j.slot][:, t0:t0 + n, :],
                                              bank16(s)[:, 0:n * P].rearrange("p (t c) -> p t c", c=P))\
                            .then_inc(sem2("at_ready")[j.slot], 1)
                        dve.wait_ge(sem2("at_ready")[j.slot], NH * j.use + c + 1)
                        dve.sem_inc(sem2("tr_free")[s], 1)
                    cols = LAST if (j.static and j.t == T - 1) else P
                    dve.wait_ge(sem("colsum"), j.n + 1)
                    nc.vector.tensor_reduce(cs_tmp[:, :], at[j.slot][:, :, 0:cols], AX.X, ALU.add).then_inc(sem("cs_tmp"), 1)
                    dve.wait_ge(sem("cs_tmp"), j.n + 1)
                    nc.vector.tensor_tensor(colsum[:, :], colsum[:, :], cs_tmp[:, :], ALU.add).then_inc(sem("colsum"), 1)
                if i.inside(T):
                    dve.wait_ge(sem2("agg_lo")[i.slot], i.use + 1)
                    dve.wait_ge(sem2("agg_used")[i.slot], i.use)
                    nc.vector.tensor_tensor(xf_sb[i.slot][:, :], bank[2 + i.slot][:, 0:D], t256[i.slot][:, 0, :], ALU.add)\
                        .then_inc(sem2("agg_sum")[i.slot], 1)
                k = i + -1
                if k.inside(T):
                    dve.wait_ge(sem("hw_psum"), k.n + 1)
                    nc.vector.scalar_tensor_tensor(out=xa[:, k.t, :], in0=b_bc, scalar=rowsum[:, k.t, :],
                                                   in1=bank[5][:, 0:D], op0=ALU.mult, op1=ALU.add).then_inc(sem("hw_done"), 1)
            adj_sweep(dve, body)
            _ = ch

        @block.tensor
        def _(pe):
            pe.wait_ge(sem("w_loaded"), 16 * 5)
            pe.wait_ge(sem("consts"), 2)
            pe.wait_ge(sem("const_chain"), 3)
            for k in range(KD):
                last = nc.tensor.transpose(bank[4][0:DA, k * P:(k + 1) * P], w1_sb[:, k, :], ident[:, :])
            last.then_inc(sem("w1t_psum"), 1)
            pe.wait_ge(sem("w1t"), 1)
            for k in range(KD):
                last = nc.tensor.matmul(bank[5][:, k * DA:(k + 1) * DA], w1t_sb[:, k, :], w2_sb, start=True, stop=True)
            last.then_inc(sem("wq_psum"), 1)
            pe.wait_ge(sem("wq"), 1)
            for u in range(2):
                pe.wait_ge(sem2("h_lo")[u], T // 2)

            def body(i):
                j, k = i + 1, i + -1
                if j.inside(T):
                    pe.wait_ge(sem2("adj16_ready")[j.slot], j.use + 1)
                    for c, (t0, n) in enumerate(HCH):
                        s, use = j.ring(NH, c)
                        pe.wait_ge(sem2("tr_free")[s], use)
                        for t in range(n):
                            last = nc.tensor.transpose(bank16(s)[:, t * P:(t + 1) * P],
                                                       adj16[j.slot][:, (t0 + t) * P:(t0 + t + 1) * P], ident16[:, :])
                        last.then_inc(sem2("tr_psum")[s], 1)
                        if c == NH - 1:
                            pe.wait_ge(sem2("tr_psum")[s], use + 1)
                            pe.sem_inc(sem2("adj16_free")[j.slot], 1)
                if k.inside(T):
                    pe.wait_ge(sem2("agg_sum")[k.slot], k.use + 1)
                    for c in range(KD):
                        last = nc.tensor.transpose(bank[4][:, c * P:(c + 1) * P], xf_sb[k.slot][:, c * P:(c + 1) * P], ident[:, :])
                    last.then_inc(sem("aggT_psum"), 1)
                if i.inside(T):
                    pe.wait_ge(sem2("at_ready")[i.slot], NH * (i.use + 1))
                    pe.wait_ge(sem2("agg_sum")[i.slot], i.use)
                    for t in range(T):
                        last = nc.tensor.matmul(bank[2 + i.slot][:, :], at[i.slot][:, t, :], parts[:, t, :],
                                                start=(t == 0), stop=(t == T - 1))
                    last.then_inc(sem2("agg_psum")[i.slot], 1)
                    pe.wait_ge(sem2("agg_psum")[i.slot], i.use + 1)
                    pe.sem_inc(sem2("at_used")[i.slot], 1)
                if k.inside(T):
                    pe.wait_ge(sem("aggT"), k.n + 1)
                    pe.sem_inc(sem2("agg_used")[k.slot], 1)
                    pe.wait_ge(sem("hw_done"), k.n)
                    for c in range(KD):
                        last = nc.tensor.matmul(bank[5][:, 0:D], zt[:, c, :], w_sb[:, c, :], start=(c == 0), stop=(c == KD - 1))
                    last.then_inc(sem("hw_psum"), 1)
            adj_sweep(pe, body)

    with nc.Block() as block:

        @block.sync
        def _(sp):
            sp.wait_ge(sem("x1"), T)
            sp.dma_start(x1_d, x_all[:, :, :].rearrange("p t d -> p (t d)")).then_inc(sem("x1_stored"), 16)
            for n, u in enumerate((U1, U2, U3)):
                sp.dma_start(u_sb[:, n, :, :], u[0].rearrange("(k p) n -> p k n", p=P)).then_inc(sem("u_loaded"), 16)
            sp.wait_ge(sem("x1_stored"), 16)
            sp.wait_ge(sem("u_loaded"), 48)

        @block.vector
        def _(dve):
            ch = Chain(dve, "mid_chain")
            ch.link(nc.vector.tensor_tensor(colsum[:, T - 1:T], colsum[:, T - 1:T], padone[:, :], ALU.add))
            ch.link(nc.vector.reciprocal(rdeg[:, :, 0], colsum[:, :]))
            ch.link(nc.vector.tensor_scalar(lt[:, :], colsum[:, :], 1.0, 1e-12, ALU.add, ALU.max))
            ch.link(nc.vector.reciprocal(cinv[:, :, 0], lt[:, :]))
            ch.link(nc.vector.tensor_scalar(lt[:, :], rowsum[:, :, 0], 1.0, 1e-12, ALU.add, ALU.max))
            ch.link(nc.vector.reciprocal(rinv[:, :, 0], lt[:, :]))
            ch.link(nc.vector.tensor_tensor(lt[:, :], lt[:, :], cinv[:, :, 0], ALU.mult))
            ch.link(nc.vector.tensor_reduce(ratio[:, :], lt[:, :], AX.X, ALU.max))
            nc.vector.tensor_scalar(ratio[:, :], ratio[:, :], 1.0, None, ALU.max).then_inc(sem("ratio"), 1)
            dve.wait_ge(sem("ratio_all"), 1)
            ch.link(nc.vector.reciprocal(kappa[:, :], ratio_all[:, :]))
            ch.link(nc.vector.tensor_scalar(rinv_s[:, :, 0], rinv[:, :, 0], 1.0 / SCALE, None, ALU.mult))
            ch.link(nc.vector.tensor_scalar(cinv_r[:, :, 0], cinv[:, :, 0], ratio_all[:, :], 1.0 / SCALE, ALU.mult, ALU.mult))
            with dve.Fori(0, T) as t:
                nc.vector.scalar_tensor_tensor(out=x_all[:, t, :], in0=xa[:, t, :], scalar=rdeg[:, t, :],
                                               in1=x_all[:, t, :], op0=ALU.mult, op1=ALU.add).then_inc(sem("x1"), 1)
            dve.wait_ge(sem("x1"), T)
            with dve.Fori(0, T) as t:
                nc.vector.bn_stats(stats[:, t, :], x_all[:, t, :]).then_inc(sem("ln_stats"), 1)
            dve.wait_ge(sem("ln_stats"), 2 * T)
            for t in range(T):
                nc.vector.bn_aggr(mv[:, t, :], stats[:, t, :]).then_inc(sem("ln_mv"), 1)
            dve.wait_ge(sem("ln_mv"), 2 * T)
            layernorm_scalars(dve, 1, 1.0)

            def body(i):
                dve.wait_ge(sem2("X_hi")[i.slot], i.use + 1)
                nc.vector.scalar_tensor_tensor(out=parts[:, i.t, D:2 * D], in0=xo_sb[i.slot][:, :], scalar=SCALE,
                                               in1=parts[:, i.t, 0:D], op0=ALU.mult, op1=ALU.subtract)\
                    .then_inc(sem2("X_lo")[i.slot], 1)
                dve.wait_ge(sem2("qk_psum")[i.slot], i.use + 1)
                nc.vector.tensor_copy(queries[0:DA, bass.ds(i.t * P, P)], bank[2 + i.slot][0:DA, 0:P])
                nc.vector.tensor_copy(keys[0:DA, bass.ds(i.t * P, P)], bank[2 + i.slot][0:DA, P:2 * P])\
                    .then_inc(sem2("qk_done")[i.slot], 1)
            sweep(dve, 0, 2, T // 2 - 1, T, body)

        @block.gpsimd
        def _(pool):
            pool.wait_ge(sem("ratio"), 1)
            nc.gpsimd.partition_all_reduce(ratio_all[:, :], ratio[:, :], P, bass.bass_isa.ReduceOp.max).then_inc(sem("ratio_all"), 1)

            def body(i):
                pool.wait_ge(sem2("X32")[i.slot], i.use + 1)
                nc.gpsimd.tensor_copy(xa[:, i.t, :], xo_sb[i.slot][:, :]).then_inc(sem2("xa_copied")[i.slot], 1)
            sweep(pool, 0, 2, T // 2 - 1, T, body)

        @block.scalar
        def _(act):
            layernorm_sqrt(act, 1)
            act.wait_ge(sem("ln_ready"), 2)

            def body(i):
                act.wait_ge(sem2("xa_copied")[i.slot], i.use)
                act.wait_ge(sem2("X_lo")[i.slot], i.use)
                act.wait_ge(sem2("XT_psum")[i.slot], i.use)
                nc.scalar.activation(xo_sb[i.slot][:, :], x_all[:, i.t, :], ACT.Relu, bias=lb[:, i.t, :], scale=ly[:, i.t, :])\
                    .then_inc(sem2("X32")[i.slot], 1)
                act.wait_ge(sem2("X32")[i.slot], i.use + 1)
                nc.scalar.activation(parts[:, i.t, 0:D], xo_sb[i.slot][:, :], ACT.Copy, scale=SCALE).then_inc(sem2("X_hi")[i.slot], 1)
                act.wait_ge(sem2("XT_psum")[i.slot], i.use + 1)
                act.wait_ge(sem2("qk_psum")[i.slot], i.use)
                nc.scalar.activation(t256[i.slot][:, 0, :], bank[i.slot][:, 0:D], ACT.Copy).then_inc(sem2("XT")[i.slot], 1)
            sweep(act, 0, 2, T // 2 - 1, T, body)

        @block.tensor
        def _(pe):
            def body(i):
                pe.wait_ge(sem2("X32")[i.slot], i.use + 1)
                pe.wait_ge(sem2("XT")[i.slot], i.use)
                for c in range(KD):
                    last = nc.tensor.transpose(bank[i.slot][:, c * P:(c + 1) * P], xo_sb[i.slot][:, c * P:(c + 1) * P], ident[:, :])
                last.then_inc(sem2("XT_psum")[i.slot], 1)
                pe.wait_ge(sem2("XT")[i.slot], i.use + 1)
                pe.wait_ge(sem2("qk_done")[i.slot], i.use)
                for n, w in enumerate((wq_sb, w3_sb)):
                    for c in range(KD):
                        last = nc.tensor.matmul(bank[2 + i.slot][0:DA, n * P:(n + 1) * P], w[:, c, :],
                                                t256[i.slot][:, 0, c * P:(c + 1) * P], start=(c == 0), stop=(c == KD - 1))
                last.then_inc(sem2("qk_psum")[i.slot], 1)
            sweep(pe, 0, 2, T // 2 - 1, T, body)

    def diffusion_step(s):
        first = s == 0
        row = slice(s * DA, (s + 1) * DA)
        q_rows = slice(0, (s + 1) * DA)

        def S(name):
            return sem(f"step_{name}")

        def S2(name):
            return sem2(f"step_{name}")

        def step_sweep(eng, body):
            sweep(eng, -1, 3, (T - 4) // 2, T + 1, body, base=s * T)

        with nc.Block() as block:

            @block.sync
            def _(sp):
                if not first:
                    sp.dma_start(xa[:, :, :], xa_d.rearrange("t p d -> p t d")).then_inc(S("xa_loaded"), 16)
                    for n, u in enumerate((U1, U2, U3)):
                        sp.dma_start(u_sb[:, n, :, :], u[s].rearrange("(k p) n -> p k n", p=P)).then_inc(S("u_loaded"), 16)

                def body(i):
                    j, k = i + 1, i + -1
                    if j.inside(T):
                        sp.wait_ge(S2("at_used")[j.slot], j.use)
                        sp.dma_start(at[j.slot][:, :, :].rearrange("p t c -> p (t c)"), adjT_d[dyn(j)])\
                            .then_inc(S2("at_loaded")[j.slot], 16)
                    if not first and i.inside(T):
                        sp.wait_ge(S2("y_done")[i.slot], i.use)
                        sp.dma_start(y_sb[i.slot][:, :], y_d[dyn(i)]).then_inc(S2("y_loaded")[i.slot], 16)
                    if first and k.inside(T):
                        sp.wait_ge(S2("xo")[k.slot], k.use + 1)
                        sp.dma_start(xa_d[dyn(k)], xo_sb[k.slot][:, :]).then_inc(S2("xo_stored")[k.slot], 16)
                        sp.wait_ge(S2("y_done")[k.slot], k.use + 1)
                        sp.dma_start(y_d[dyn(k)], y_sb[k.slot][:, :]).then_inc(S2("y_stored")[k.slot], 16)
                step_sweep(sp, body)
                if first:
                    for u in range(2):
                        sp.wait_ge(S2("xo_stored")[u], 16 * (T // 2))
                        sp.wait_ge(S2("y_stored")[u], 16 * (T // 2))

            @block.gpsimd
            def _(pool):
                if first:
                    for u in range(2):
                        nc.gpsimd.memset(pb[u][:, N:NP], 0.0).then_inc(S("p_pad"), 1)

                def body(i):
                    j, k = i + 1, i + -1
                    if j.inside(T):
                        pool.wait_ge(S2("logits_done")[j.slot], NL * j.use)
                        nc.gpsimd.tensor_copy(qs[j.slot][q_rows, :], queries[q_rows, bass.ds(j.t * P, P)]).then_inc(S2("q_ready")[j.slot], 1)
                        pool.wait_ge(S2("at_loaded")[j.slot], 16 * (j.use + 1))
                        nc.gpsimd.tensor_tensor(at[j.slot][:, j.t, :], at[j.slot][:, j.t, :], ident16[:, :], ALU.add)\
                            .then_inc(S2("st_ready")[j.slot], 1)
                    if first and k.inside(T):
                        pool.wait_ge(S2("fb_hi")[k.slot], 3 * (k.use + 1))
                        nc.gpsimd.tensor_tensor(parts_fb[:, k.t, D:2 * D], xf_sb[k.slot][:, :], parts_fb[:, k.t, 0:D], ALU.subtract)\
                            .then_inc(S2("fb_lo")[k.slot], 1)
                        nc.gpsimd.tensor_tensor(parts_fb[:, k.t, 3 * D:4 * D], xk_sb[:, :], parts_fb[:, k.t, 2 * D:3 * D], ALU.subtract)\
                            .then_inc(S2("fb_lo")[k.slot], 1)
                step_sweep(pool, body)

            @block.scalar
            def _(act):
                def body(i):
                    j, k = i + 1, i + -1
                    if k.inside(T):
                        for c, (t0, n) in enumerate(TCH):
                            sl, use = k.ring(NT, c)
                            act.wait_ge(S2("pt_psum")[sl], use + 1)
                            act.wait_ge(S2("pt_used")[sl], use)
                            nc.scalar.activation(pt[sl][:, 0:n * P], bank[2 + sl][:, 0:n * P], ACT.Copy).then_inc(S2("pt")[sl], 1)
                        if first:
                            act.wait_ge(S2("xfb")[k.slot], 2 * (k.use + 1))
                            nc.scalar.activation(parts_fb[:, k.t, 0:D], xf_sb[k.slot][:, :], ACT.Copy).then_inc(S2("fb_hi")[k.slot], 1)
                            act.wait_ge(S2("fb_lo")[1 - k.slot], 2 * (k + 1).use)
                            nc.scalar.activation(xk_sb[:, :], xb_sb[k.slot][:, :], ACT.Copy, scale=kappa[:, :]).then_inc(S2("fb_hi")[k.slot], 1)
                            act.wait_ge(S2("fb_hi")[k.slot], 3 * k.use + 2)
                            nc.scalar.activation(parts_fb[:, k.t, 2 * D:3 * D], xk_sb[:, :], ACT.Copy).then_inc(S2("fb_hi")[k.slot], 1)
                        act.wait_ge(S("fbT_psum"), k.n + 1)
                        act.wait_ge(S("z_psum"), k.n)
                        nc.scalar.activation(zt[:, 0:4, :].rearrange("p k c -> p (k c)"), bank[7][:, :], ACT.Copy,
                                             scale=(1.0 / SCALE if first else 1.0)).then_inc(S("fbT"), 1)
                        act.wait_ge(S("px_psum"), k.n + 1)
                        act.wait_ge(S2("xoT_psum_of")[k.slot], k.use)
                        if first:
                            act.wait_ge(S2("xo_stored")[k.slot], 16 * k.use)
                        nc.scalar.activation(xo_sb[k.slot][:, :], bank[4][:, 0:D], ACT.Copy, scale=rkept[k.slot][:, :])\
                            .then_inc(S2("xo")[k.slot], 1)
                    if j.inside(T):
                        act.wait_ge(S("p_pad"), 2)
                        act.wait_ge(S2("p_used")[j.slot], j.use)
                        for c, (c0, w) in enumerate(LCH):
                            sl, use = j.ring(NL, c)
                            act.wait_ge(S2("logits_psum")[sl], use + 1)
                            nc.scalar.activation(pb[j.slot][:, c0:c0 + w], bank[sl][:, 0:w], ACT.Copy).then_inc(S2("logits_done")[j.slot], 1)
                            act.wait_ge(S2("logits_done")[j.slot], NL * j.use + c + 1)
                            act.sem_inc(S2("logits_free")[sl], 1)
                    if k.inside(T):
                        act.wait_ge(S("xoT_psum"), k.n + 1)
                        nc.scalar.activation(zt[:, 4:6, :].rearrange("p k c -> p (k c)"), bank[7][:, 0:D], ACT.Copy).then_inc(S("xoT"), 1)
                    if i.inside(T):
                        act.wait_ge(S("sx_psum"), i.n + 1)
                        if first:
                            for n, sc in enumerate((rinv, cinv)):
                                nc.scalar.activation(t256[i.slot][:, n, :], bank[5][:, D:2 * D], ACT.Copy, scale=sc[:, i.t, :])\
                                    .then_inc(S2("sx_lo")[i.slot], 1)
                        else:
                            for n, sc in enumerate((rinv_s, cinv_r)):
                                nc.scalar.activation(t256[i.slot][:, n, :], bank[5 + n][:, D:2 * D], ACT.Copy, scale=sc[:, i.t, :])\
                                    .then_inc(S2("sx_lo")[i.slot], 1)
                    if first and k.inside(T):
                        act.wait_ge(S("z_psum"), k.n + 1)
                        r1 = slice(DA, 2 * DA)
                        nc.scalar.activation(queries[r1, bass.ds(k.t * P, P)], bank[7][0:DA, D:D + P], ACT.Copy)
                        nc.scalar.activation(keys[r1, bass.ds(k.t * P, P)], bank[7][0:DA, D + P:D + 2 * P], ACT.Copy)\
                            .then_inc(S("qk_done"), 1)
                    if j.inside(T):
                        act.wait_ge(S2("negmax")[j.slot], j.use + 1)
                        nc.scalar.activation(pb[j.slot][:, 0:N], pb[j.slot][:, 0:N], ACT.Exp, bias=negmax[j.slot][:, :],
                                             accum_out=zsum[j.slot][:, :]).then_inc(S2("p_ready")[j.slot], 1)
                step_sweep(act, body)

            @block.vector
            def _(dve):
                if not first:
                    pass

                def body(i):
                    j, k = i + 1, i + -1
                    LINKS = 2 * EVALS + 2 + EVALS - 0
                    if i.inside(T):
                        p = pb[i.slot][:, 0:N]
                        ch = Chain(dve, "step_search", base=i.n * LINKS)
                        dve.wait_ge(S2("p_ready")[i.slot], i.use + 1)
                        ch.link(nc.vector.tensor_scalar(target[:, :], zsum[i.slot][:, :], NUCLEUS, None, ALU.mult))
                        ch.link(nc.vector.memset(thr[:, :], math.exp(-RANGE / 2)))
                        for e in range(EVALS):
                            ch.link(nc.vector.scalar_tensor_tensor(out=junk[:, 0:N], in0=p, scalar=thr[:, :], in1=p,
                                                                   op0=ALU.is_ge, op1=ALU.mult, accum_out=mass[:, :]))
                            d = RANGE / 2 ** (e + 2)
                            up, down = (math.exp(d), math.exp(-d)) if e < EVALS - 1 else (1 - 4e-6, (1 - 4e-6) * math.exp(-2 * d))
                            ch.link(nc.vector.tensor_scalar(step_up[:, :], mass[:, :], target[:, :], up - down, ALU.is_ge, ALU.mult))
                            ch.link(nc.vector.scalar_tensor_tensor(out=thr[:, :], in0=step_up[:, :], scalar=down, in1=thr[:, :],
                                                                   op0=ALU.add, op1=ALU.mult))
                        assert ch.count == LINKS
                    if j.inside(T):
                        dve.wait_ge(S2("logits_done")[j.slot], NL * (j.use + 1))
                        nc.vector.tensor_reduce(negmax[j.slot][:, :], pb[j.slot][:, 0:N], AX.X, ALU.max, negate=True)\
                            .then_inc(S2("negmax")[j.slot], 1)
                    if i.inside(T):
                        nc.vector.scalar_tensor_tensor(out=p, in0=p, scalar=thr[:, :], in1=p, op0=ALU.is_ge, op1=ALU.mult,
                                                       accum_out=kept[:, :]).then_inc(S2("masked")[i.slot], 1)
                        dve.wait_ge(S2("masked")[i.slot], i.use + 1)
                        dve.wait_ge(S2("xo")[i.slot], i.use)
                        nc.vector.reciprocal(rkept[i.slot][:, :], kept[:, :]).then_inc(S2("rkept")[i.slot], 1)
                        dve.wait_ge(S2("sx_lo")[i.slot], 2 * (i.use + 1))
                        if first:
                            dve.wait_ge(S2("fb_lo")[i.slot], 2 * i.use)
                        dve.wait_ge(S2("fbT_psum_of")[i.slot], i.use)
                        for n, (dst, sc) in enumerate(((xf_sb, rinv if first else rinv_s), (xb_sb, cinv if first else cinv_r))):
                            nc.vector.scalar_tensor_tensor(out=dst[i.slot][:, :], in0=bank[5 if first else 5 + n][:, 0:D],
                                                           scalar=sc[:, i.t, :], in1=t256[i.slot][:, n, :],
                                                           op0=ALU.mult, op1=ALU.add).then_inc(S2("xfb")[i.slot], 1)
                    if k.inside(T):
                        dve.wait_ge(S("z_psum"), k.n + 1)
                        if first:
                            dve.wait_ge(S("qk_done"), k.n + 1)
                            dve.wait_ge(S2("y_stored")[k.slot], 16 * k.use)
                            nc.vector.tensor_tensor(y_sb[k.slot][:, :], bank[7][:, 0:D], xa[:, k.t, :], ALU.add).then_inc(S2("y_done")[k.slot], 1)
                        else:
                            dve.wait_ge(S2("y_loaded")[k.slot], 16 * (k.use_here + 1))
                            nc.vector.tensor_tensor(yall[:, k.t, :], bank[7][:, 0:D], y_sb[k.slot][:, :], ALU.add).then_inc(S2("y_done")[k.slot], 1)
                step_sweep(dve, body)

            @block.tensor
            def _(pe):
                if not first:
                    pe.wait_ge(S("xa_loaded"), 16)
                    pe.wait_ge(S("u_loaded"), 48)

                def body(i):
                    j, k = i + 1, i + -1
                    if k.inside(T):
                        pe.wait_ge(S2("masked")[k.slot], k.use + 1)
                        pe.wait_ge(S("p_pad"), 2)

                        def transposes(c):
                            t0, n = TCH[c]
                            sl, use = k.ring(NT, c)
                            pe.wait_ge(S2("pt")[sl], use)
                            for t in range(n):
                                last = nc.tensor.transpose(bank[2 + sl][:, t * P:(t + 1) * P],
                                                           pb[k.slot][:, (t0 + t) * P:(t0 + t + 1) * P], ident[:, :])
                            last.then_inc(S2("pt_psum")[sl], 1)

                        def product(c):
                            t0, n = TCH[c]
                            sl, use = k.ring(NT, c)
                            pe.wait_ge(S2("pt")[sl], use + 1)
                            for t in range(n):
                                last = nc.tensor.matmul(bank[4][:, 0:D], pt[sl][:, t * P:(t + 1) * P], xa[:, t0 + t, :],
                                                        start=(t0 + t == 0), stop=(t0 + t == T - 1))
                            last.then_inc(S2("pt_used")[sl], 1)

                        transposes(0)
                        pe.wait_ge(S2("xo")[1 - k.slot], (k + 1).use)
                        for c in range(NT):
                            if c + 1 < NT:
                                transposes(c + 1)
                            product(c)
                        sl, use = k.ring(NT, NT - 1)
                        pe.wait_ge(S2("pt_used")[sl], use + 1)
                        pe.sem_inc(S2("p_used")[k.slot], 1)
                        pe.sem_inc(S("px_psum"), 1)
                        pe.wait_ge(S2("xfb")[k.slot], 2 * (k.use + 1))
                        pe.wait_ge(S2("y_done")[1 - k.slot], (k + 1).use)
                        if first:
                            pe.wait_ge(S("qk_done"), k.n)
                        for n, src in enumerate((xf_sb, xb_sb)):
                            for c in range(KD):
                                q = n * KD + c
                                last = nc.tensor.transpose(bank[7][:, q * P:(q + 1) * P], src[k.slot][:, c * P:(c + 1) * P], ident[:, :])
                        last.then_inc(S("fbT_psum"), 1)
                        pe.wait_ge(S("fbT_psum"), k.n + 1)
                        pe.sem_inc(S2("fbT_psum_of")[k.slot], 1)
                    if j.inside(T):
                        pe.wait_ge(S2("q_ready")[j.slot], j.use + 1)
                        for c, (c0, w) in enumerate(LCH):
                            sl, use = j.ring(NL, c)
                            pe.wait_ge(S2("logits_free")[sl], use)
                            nc.tensor.matmul(bank[sl][:, 0:w], qs[j.slot][row, :], keys[row, c0:c0 + w], start=True, stop=True)\
                                .then_inc(S2("logits_psum")[sl], 1)
                    if k.inside(T):
                        pe.wait_ge(S2("xo")[k.slot], k.use + 1)
                        pe.wait_ge(S("fbT"), k.n + 1)
                        for c in range(KD):
                            last = nc.tensor.transpose(bank[7][:, c * P:(c + 1) * P], xo_sb[k.slot][:, c * P:(c + 1) * P], ident[:, :])
                        last.then_inc(S("xoT_psum"), 1)
                        pe.wait_ge(S("xoT_psum"), k.n + 1)
                        pe.sem_inc(S2("xoT_psum_of")[k.slot], 1)
                    if i.inside(T):
                        pe.wait_ge(S2("st_ready")[i.slot], i.use + 1)
                        pe.wait_ge(S2("xfb")[1 - i.slot], 2 * (i + 1).use)
                        for n in range(1 if first else 2):
                            for t in range(T):
                                mov = parts[:, t, :] if first else parts_fb[:, t, n * 2 * D:(n + 1) * 2 * D]
                                last = nc.tensor.matmul(bank[5 + n][:, :], at[i.slot][:, t, :], mov, start=(t == 0), stop=(t == T - 1))
                        last.then_inc(S("sx_psum"), 1)
                        pe.wait_ge(S("sx_psum"), i.n + 1)
                        pe.sem_inc(S2("at_used")[i.slot], 1)
                    if k.inside(T):
                        pe.wait_ge(S("xoT"), k.n + 1)
                        for q in range(6):
                            last = nc.tensor.matmul(bank[7][:, 0:D], zt[:, q, :], u_sb[:, q // KD, q % KD, :],
                                                    start=(q == 0), stop=(q == 5))
                        if first:
                            for n, w in enumerate((wq_sb, w3_sb)):
                                for c in range(KD):
                                    last = nc.tensor.matmul(bank[7][0:DA, D + n * P:D + (n + 1) * P], w[:, c, :], zt[:, 4 + c, :],
                                                            start=(c == 0), stop=(c == KD - 1))
                        last.then_inc(S("z_psum"), 1)
                step_sweep(pe, body)

    diffusion_step(0)
    diffusion_step(1)

    with nc.Block() as block:

        @block.sync
        def _(sp):
            sp.dma_start(xa[:, :, :].rearrange("p t d -> p (t d)"), x1_d).then_inc(sem("x1_loaded"), 16)
            sp.dma_start(gamma_bc, bc(gamma)).then_inc(sem("x1_loaded"), 16)
            sp.dma_start(beta_bc, bc(beta)).then_inc(sem("x1_loaded"), 16)

            def body(i):
                sp.wait_ge(sem2("o_done")[i.slot], i.use + 1)
                sp.dma_start(out_t[dyn(i)], xo_sb[i.slot][:, :]).then_inc(sem2("o_stored")[i.slot], 16)
            out_t = out[0:(T - 1) * P, :].rearrange("(t p) n -> t p n", p=P)
            sweep(sp, 0, 2, (T - 1) // 2 - 1, T - 1, body)
            i = Idx(0, T - 1)
            sp.wait_ge(sem2("o_done")[i.slot], i.use + 1)
            even = LAST - LAST % 16
            for r0, r1 in ((0, even), (even, LAST)):
                if r1 > r0:
                    sp.dma_start(out[(T - 1) * P + r0:(T - 1) * P + r1, :], xo_sb[i.slot][r0:r1, :]).then_inc(sem("o_last_stored"), 16)
            sp.wait_ge(sem("o_last_stored"), 16 * (2 if LAST % 16 and LAST > 16 else 1))
            sp.wait_ge(sem2("o_stored")[0], 16 * (T // 2))
            sp.wait_ge(sem2("o_stored")[1], 16 * (T // 2 - 1))

        @block.scalar
        def _(act):
            layernorm_sqrt(act, 2)
            act.wait_ge(sem("ln_ready"), 3)

            def body(i):
                act.wait_ge(sem2("o_done")[i.slot], i.use)
                nc.scalar.activation(xf_sb[i.slot][:, :], yall[:, i.t, :], ACT.Identity, bias=lb[:, i.t, :], scale=ly[:, i.t, :])\
                    .then_inc(sem2("o_norm")[i.slot], 1)
            sweep(act, 0, 2, T // 2 - 1, T, body)

        @block.vector
        def _(dve):
            with dve.Fori(0, T) as t:
                nc.vector.bn_stats(stats[:, t, :], yall[:, t, :]).then_inc(sem("ln_stats"), 1)
            dve.wait_ge(sem("ln_stats"), 3 * T)
            for t in range(T):
                nc.vector.bn_aggr(mv[:, t, :], stats[:, t, :]).then_inc(sem("ln_mv"), 1)
            dve.wait_ge(sem("ln_mv"), 3 * T)
            layernorm_scalars(dve, 2, 1.0)
            dve.wait_ge(sem("x1_loaded"), 48)

            def body(i):
                ch = Chain(dve, "out_chain", base=2 * i.n)
                dve.wait_ge(sem2("o_norm")[i.slot], i.use + 1)
                ch.link(nc.vector.tensor_tensor(xb_sb[i.slot][:, :], xf_sb[i.slot][:, :], gamma_bc, ALU.mult))
                ch.link(nc.vector.tensor_tensor(xb_sb[i.slot][:, :], xb_sb[i.slot][:, :], beta_bc, ALU.add))
                dve.wait_ge(sem2("o_stored")[i.slot], 16 * i.use)
                nc.vector.tensor_tensor(xo_sb[i.slot][:, :], xb_sb[i.slot][:, :], xa[:, i.t, :], ALU.add).then_inc(sem2("o_done")[i.slot], 1)
            sweep(dve, 0, 2, T // 2 - 1, T, body)


_INS = ["x", "adj", "L0_gnn_W", "L0_gnn_b", "L1_gnn_W1", "L1_gnn_W2", "L1_gnn_W3",
        "L1_gnn_U1", "L1_gnn_U2", "L1_gnn_U3", "L1_gnn_gamma", "L1_gnn_beta"]


def kernel(**inputs):
    import numpy as _np
    import concourse.bacc as _bacc
    from concourse import mybir as _mybir
    from concourse.bass_utils import run_bass_kernel_spmd as _run

    nc = _bacc.Bacc("TRN2", target_bir_lowering=False, num_devices=1)
    arrays, args = {}, []
    for name in _INS:
        a = _np.ascontiguousarray(inputs[name])
        arrays[f"in_{name}_dram"] = a
        args.append(nc.dram_tensor(f"in_{name}_dram", a.shape, _mybir.dt.from_np(a.dtype), kind="ExternalInput").ap())
    o = nc.dram_tensor("out_0_dram", inputs["x"].shape, _mybir.dt.float32, kind="ExternalOutput").ap()
    gnn_program(nc, *args, o)
    r = _run(nc, [arrays], core_ids=[0])
    return r.results[0]["out_0_dram"]
```

```python
import math

import numpy as np
import concourse.bass as bass
from concourse import mybir


class Idx:

    def __init__(self, g, off, base=0):
        self.g, self.off, self.base = g, off, base
        self.static = isinstance(g, int)
        self.t = 2 * g + off
        self.n = 2 * g + (off + base)
        self.slot = off % 2
        self.use = g + (off + base) // 2
        self.use_here = g + off // 2

    def __add__(self, d):
        return Idx(self.g, self.off + d, self.base)

    def inside(self, tiles):
        return not self.static or 0 <= self.t < tiles

    def ring(self, per, c):
        s = per * (self.off + self.base) + c
        return s % 2, per * self.g + s // 2


def gnn_program(nc, x, adj, W, b, W1, W2, W3, U1, U2, U3, gamma, beta, out):
    f32, f16, i32 = mybir.dt.float32, mybir.dt.float16, mybir.dt.int32
    ALU, ACT, AX = mybir.AluOpType, mybir.ActivationFunctionType, mybir.AxisListType

    P = 128
    N, D = x.shape
    DA = W2.shape[0]
    KD = D // P
    T = -(-N // P)
    NP = T * P
    LAST = N - (T - 1) * P
    EPS = 1e-5
    SCALE = 1024.0
    NUCLEUS = 0.9
    CW = 512
    LCH = [(c, min(CW, N - c)) for c in range(0, N, CW)]
    TCH = [(c, min(4, T - c)) for c in range(0, T, 4)]
    HCH = [(c, min(8, T - c)) for c in range(0, T, 8)]
    NL, NT, NH = len(LCH), len(TCH), len(HCH)
    RANGE = math.log(N / (1 - NUCLEUS)) + 0.01
    SEARCH = ((5, 2, 2.5), (6, 3, 4.0))
    KMAX = 2 + max(b for b, _, _ in SEARCH)
    ROUNDS = (3, 8, -(-N // 8))
    LOOKS = len(ROUNDS)
    BIG = 2.0 ** 40
    TAKE = 6
    LINKS = [1 + 3 * b - 2 + 10 + 7 * n + 1 + TAKE for b, n, _ in SEARCH]

    adjT_d = nc.dram_tensor("adjT_d", [T, P, T * P], f16, kind="Internal").ap()
    q_d = nc.dram_tensor("q_d", [2, T, DA, P], f32, kind="Internal").ap()
    x1_d = nc.dram_tensor("x1_d", [P, T * D], f32, kind="Internal").ap()
    y_d = nc.dram_tensor("y_d", [T, P, D], f32, kind="Internal").ap()
    xa_d = nc.dram_tensor("xa_d", [T, P, D], f32, kind="Internal").ap()

    def sb(name, shape, dt):
        return nc.alloc_sbuf_tensor(name, shape, dt)

    sem_names = {}

    def sem(name):
        if name not in sem_names:
            sem_names[name] = nc.alloc_semaphore(name)
        return sem_names[name]

    def sem2(name):
        return [sem(f"{name}_{u}") for u in range(2)]


    regA = sb("regA", [P, T * D], f32)
    regB = sb("regB", [P, T * 2 * D], f32)
    xa = sb("xa", [P, T, D], f32)
    keys = sb("keys", [P, NP], f32)
    at = [sb(f"at{u}", [P, T, P], f16) for u in range(2)]
    pb_all = sb("pb_all", [P, 2 * NP], f32)
    pb = [pb_all[:, u * NP:(u + 1) * NP] for u in range(2)]
    below = sb("below", [P, N + 8], f32)
    pt = [sb(f"pt{u}", [P, CW], f32) for u in range(2)]
    parts = regA[:, :].bitcast(f16).rearrange("p (t c) -> p t c", c=2 * D)
    yall = regA[:, :].rearrange("p (t d) -> p t d", d=D)
    parts_fb = regB[:, :].bitcast(f16).rearrange("p (t c) -> p t c", c=4 * D)
    adj_in = [regB[:, u * NP:(u + 1) * NP] for u in range(2)]
    adj16 = [regB[:, (2 * NP + u * NP // 2):(2 * NP + (u + 1) * NP // 2)].bitcast(f16) for u in range(2)]
    x_all = pb_all[:, :].rearrange("p (t d) -> p t d", d=D)

    ident = sb("ident", [P, P], f32)
    ident16 = sb("ident16", [P, P], f16)
    padone = sb("padone", [P, 1], f32)
    early = below[:, :]
    w_sb = early[:, 0:KD * D].rearrange("p (k d) -> p k d", d=D)
    b_bc = early[:, KD * D:(KD + 1) * D]
    e0 = (KD + 1) * D
    w1_sb = early[:, e0:e0 + KD * DA].rearrange("p (k d) -> p k d", d=DA)
    w1t_sb = early[0:DA, e0 + KD * DA:e0 + KD * (DA + P)].rearrange("p (k d) -> p k d", d=P)
    w2_sb = early[0:DA, e0 + KD * (DA + P):e0 + KD * (DA + P) + DA]
    gamma_bc = keys[:, 0:D]
    beta_bc = keys[:, D:2 * D]
    wq_sb = sb("wq_sb", [P, KD, DA], f32)
    w3_sb = sb("w3_sb", [P, KD, DA], f32)
    u_sb = sb("u_sb", [P, 3, KD, D], f32)
    stats = sb("stats", [P, T, 6], f32)
    mv = sb("mv", [P, T, 2], f32)
    ve = sb("ve", [P, T], f32)
    sd = sb("sd", [P, T], f32)
    lt = sb("lt", [P, T], f32)
    ly = sb("ly", [P, T, 1], f32)
    lb = sb("lb", [P, T, 1], f32)
    rowsum = sb("rowsum", [P, T, 1], f32)
    colsum = sb("colsum", [P, T], f32)
    cs_tmp = sb("cs_tmp", [P, T], f32)
    rdeg = sb("rdeg", [P, T, 1], f32)
    rinv = sb("rinv", [P, T, 1], f32)
    cinv = sb("cinv", [P, T, 1], f32)
    cinv_r = sb("cinv_r", [P, T, 1], f32)
    rinv_s = sb("rinv_s", [P, T, 1], f32)
    ratio = sb("ratio", [P, 1], f32)
    ratio_all = sb("ratio_all", [P, 1], f32)
    kappa = sb("kappa", [P, 1], f32)
    t256 = [sb(f"t256_{u}", [P, 2, D], f32) for u in range(2)]
    xf_sb = [sb(f"xf_sb{u}", [P, D], f32) for u in range(2)]
    xb_sb = [sb(f"xb_sb{u}", [P, D], f32) for u in range(2)]
    xo_sb = [sb(f"xo_sb{u}", [P, D], f32) for u in range(2)]
    xk_sb = sb("xk_sb", [P, D], f32)
    zt = sb("zt", [P, 6, P], f32)
    y_sb = [sb(f"y_sb{u}", [P, D], f32) for u in range(2)]
    qs = [sb(f"qs{u}", [P, P], f32) for u in range(2)]
    qo = sb("qo", [DA, P], f32)
    negmax = [sb(f"negmax{u}", [P, 1], f32) for u in range(2)]
    thr = [sb(f"thr{u}", [P, KMAX], f32) for u in range(2)]
    mass = [sb(f"mass{u}", [P, KMAX], f32) for u in range(2)]
    target = sb("target", [P, 1], f32)
    pad_target = sb("pad_target", [P, 1], f32)
    factor = sb("factor", [P, 1], f32)
    is_lo = sb("is_lo", [P, KMAX], f32)
    wk = sb("wk", [P, KMAX], f32)
    lo = sb("lo", [P, 2], f32)
    hi = sb("hi", [P, 2], f32)
    cur = sb("cur", [P, 2], f32)
    m_lo = sb("m_lo", [P, 1], i32)
    m_hi = sb("m_hi", [P, 1], i32)
    frac = sb("frac", [P, 4], f32)
    ones8 = sb("ones8", [P, 8], f32)
    top8 = sb("top8", [P, 8], f32)
    take8 = sb("take8", [P, 8], f32)
    run9 = sb("run9", [P, 9], f32)
    run8 = sb("run8", [P, 8], f32)
    unsettled = sb("unsettled", [P, 1], f32)
    any_un = sb("any_un", [P, LOOKS], f32)
    tick = sb("tick", [1, 1 + LOOKS], f32)
    pool_tick = sb("pool_tick", [P, LOOKS], f32)
    rkept = [sb(f"rkept{u}", [P, 1], f32) for u in range(2)]

    bank = [nc.alloc_psum_tensor(f"bank{i}", [P, CW], f32) for i in range(8)]

    def bank16(i):
        return bank[i][:, :].bitcast(f16)

    class Chain:

        def __init__(self, eng, name, base=0):
            self.eng, self.sem, self.base, self.count = eng, sem(name), base, 0

        def link(self, ins, hold=False):
            self.count += 1
            ins.then_inc(self.sem, 1)
            self.eng.wait_ge(self.sem, self.base + self.count)
            if hold:
                nc.vector.memset(tick[:, 0:1], 0.0)

    def layernorm_scalars(dve, call, scale):
        ch = Chain(dve, "ln_chain", base=7 * call)
        ch.link(nc.vector.tensor_scalar(ve[:, :], mv[:, :, 1], EPS, None, ALU.add))
        ch.eng.sem_inc(sem("ln_var"), 1)
        dve.wait_ge(sem("ln_sqrt"), call + 1)
        ch.link(nc.vector.reciprocal(sd[:, :], sd[:, :]))
        ch.link(nc.vector.tensor_tensor(lt[:, :], sd[:, :], sd[:, :], ALU.mult))
        ch.link(nc.vector.tensor_tensor(lt[:, :], lt[:, :], ve[:, :], ALU.mult))
        ch.link(nc.vector.tensor_scalar(lt[:, :], lt[:, :], -0.5 * scale, 1.5 * scale, ALU.mult, ALU.add))
        ch.link(nc.vector.tensor_tensor(ly[:, :, 0], sd[:, :], lt[:, :], ALU.mult))
        ch.link(nc.vector.tensor_tensor(lt[:, :], mv[:, :, 0], ly[:, :, 0], ALU.mult))
        nc.vector.tensor_scalar(lb[:, :, 0], lt[:, :], -1.0, None, ALU.mult).then_inc(sem("ln_ready"), 1)

    def layernorm_sqrt(act, call):
        act.wait_ge(sem("ln_var"), call + 1)
        nc.scalar.activation(sd[:, :], ve[:, :], ACT.Sqrt).then_inc(sem("ln_sqrt"), 1)

    def sweep(eng, first, loop_from, pairs, last, body, base=0):
        for i in range(first, loop_from):
            body(Idx(0, i, base))
        with eng.Fori(0, pairs) as g:
            for u in range(2):
                body(Idx(g, loop_from + u, base))
        for i in range(loop_from + 2 * pairs, last):
            body(Idx(0, i, base))

    def dyn(i):
        return i.t

    def adj_sweep(eng, body):
        sweep(eng, -2, 3, (T - 6) // 2, T + 1, body)

    def bc(v):
        return v.partition_broadcast(P)

    XH = T // 2
    with nc.Block() as block:

        @block.sync
        def _(sp):
            sp.wait_ge(sem("x_pad_clear"), 1)
            sp.dma_start(x_all[:, 0:XH, :], x[0:XH * P, :].rearrange("(t p) d -> p t d", p=P)).then_inc(sem("x_loaded"), 16)
            sp.dma_start(x_all[:, XH:T - 1, :], x[XH * P:(T - 1) * P, :].rearrange("(t p) d -> p t d", p=P)).then_inc(sem("x_loaded"), 16)
            even = LAST - LAST % 16
            for r0, r1 in ((0, even), (even, LAST)):
                if r1 > r0:
                    sp.dma_start(x_all[r0:r1, T - 1, :], x[(T - 1) * P + r0:(T - 1) * P + r1, :]).then_inc(sem("x_loaded"), 16)
            sp.dma_start(w_sb[:, :, :], W.rearrange("(k p) n -> p k n", p=P)).then_inc(sem("w_loaded"), 16)
            sp.dma_start(b_bc, bc(b)).then_inc(sem("w_loaded"), 16)
            sp.dma_start(w1_sb[:, :, :], W1.rearrange("(k p) n -> p k n", p=P)).then_inc(sem("w_loaded"), 16)
            sp.dma_start(w3_sb[:, :, :], W3.rearrange("(k p) n -> p k n", p=P)).then_inc(sem("w_loaded"), 16)
            sp.dma_start(w2_sb, W2).then_inc(sem("w_loaded"), 16)

            def body(i):
                j = i + 2
                if j.inside(T):
                    sp.wait_ge(sem2("adj_in_free")[j.slot], j.use)
                    if j.static and j.t == T - 1:
                        for r0, r1 in ((0, even), (even, LAST)):
                            if r1 > r0:
                                sp.dma_start(adj_in[j.slot][r0:r1, 0:N], adj[(T - 1) * P + r0:(T - 1) * P + r1, :])\
                                    .then_inc(sem("adj_last_loaded"), 16)
                    else:
                        sp.dma_start(adj_in[j.slot][:, 0:N], adj_t[dyn(j)]).then_inc(sem2("adj_loaded")[j.slot], 16)
                if i.inside(T):
                    sp.wait_ge(sem2("at_ready")[i.slot], NH * (i.use + 1))
                    sp.dma_start(adjT_d[dyn(i)], at[i.slot][:, :, :].rearrange("p t c -> p (t c)"))\
                        .then_inc(sem2("at_stored")[i.slot], 16)

            adj_t = adj[0:(T - 1) * P, :].rearrange("(t p) n -> t p n", p=P)
            adj_sweep(sp, body)
            for u in range(2):
                sp.wait_ge(sem2("at_stored")[u], 16 * (T // 2))

        @block.gpsimd
        def _(pool):
            nc.gpsimd.memset(ident[:, :], 0.0).then_inc(sem("const_chain"), 1)
            nc.gpsimd.memset(padone[:, :], 1.0).then_inc(sem("const_chain"), 1)
            for u in range(2):
                nc.gpsimd.memset(adj_in[u][:, N:NP], 0.0).then_inc(sem("adj_pad"), 1)
            pool.wait_ge(sem("const_chain"), 2)
            nc.gpsimd.affine_select(out=ident[:, :], in_=ident[:, :], compare_op=ALU.not_equal, fill=1.0, base=0,
                                    pattern=[[-1, P]], channel_multiplier=1).then_inc(sem("const_chain"), 1)
            nc.gpsimd.affine_select(out=padone[:, :], in_=padone[:, :], compare_op=ALU.is_ge, fill=0.0, base=-LAST,
                                    pattern=[[0, 1]], channel_multiplier=1).then_inc(sem("consts"), 1)
            pool.wait_ge(sem("const_chain"), 3)
            nc.gpsimd.tensor_copy(ident16[:, :], ident[:, :]).then_inc(sem("consts"), 1)

            def low(i):
                pool.wait_ge(sem2("norm_hi")[i.slot], i.use + 1)
                nc.gpsimd.tensor_tensor(parts[:, i.t, D:2 * D], xo_sb[i.slot][:, :], parts[:, i.t, 0:D], ALU.subtract)\
                    .then_inc(sem2("norm_lo")[i.slot], 1)
            sweep(pool, 0, 2, T // 2 - 1, T, low)

        @block.scalar
        def _(act):
            layernorm_sqrt(act, 0)
            act.wait_ge(sem("ln_ready"), 1)

            def split(i):
                act.wait_ge(sem2("norm_lo")[i.slot], i.use)
                nc.scalar.activation(xo_sb[i.slot][:, :], x_all[:, i.t, :], ACT.Relu, bias=lb[:, i.t, :], scale=ly[:, i.t, :])\
                    .then_inc(sem2("normed")[i.slot], 1)
                act.wait_ge(sem2("normed")[i.slot], i.use + 1)
                nc.scalar.activation(parts[:, i.t, 0:D], xo_sb[i.slot][:, :], ACT.Copy).then_inc(sem2("norm_hi")[i.slot], 1)
            sweep(act, 0, 2, T // 2 - 1, T, split)
            act.wait_ge(sem("w1t_psum"), 1)
            nc.scalar.activation(w1t_sb[:, :, :].rearrange("p k c -> p (k c)"), bank[4][0:DA, 0:KD * P], ACT.Copy).then_inc(sem("w1t"), 1)
            act.wait_ge(sem("wq_psum"), 1)
            nc.scalar.activation(wq_sb[:, :, :].rearrange("p k c -> p (k c)"), bank[5][:, 0:KD * DA], ACT.Copy).then_inc(sem("wq"), 1)
            act.wait_ge(sem("adj_pad"), 2)

            def body(i):
                j = i + 2
                if j.inside(T):
                    if j.static and j.t == T - 1:
                        act.wait_ge(sem("adj_last_loaded"), 16 * (2 if LAST % 16 and LAST > 16 else 1))
                    else:
                        act.wait_ge(sem2("adj_loaded")[j.slot], 16 * (j.use + 1))
                    act.wait_ge(sem2("adj16_free")[j.slot], j.use)
                    nc.scalar.activation(adj16[j.slot], adj_in[j.slot], ACT.Copy, accum_out=rowsum[:, j.t, :])\
                        .then_inc(sem2("adj16_ready")[j.slot], 1)
                    act.wait_ge(sem2("adj16_ready")[j.slot], j.use + 1)
                    act.sem_inc(sem2("adj_in_free")[j.slot], 1)
                k = i + -1
                if k.inside(T):
                    act.wait_ge(sem("aggT_psum"), k.n + 1)
                    nc.scalar.activation(zt[:, 0:KD, :], bank[4][:, 0:KD * P].rearrange("p (k c) -> p k c", c=P), ACT.Copy,
                                         scale=1.0 / SCALE).then_inc(sem("aggT"), 1)
                if i.inside(T):
                    act.wait_ge(sem2("agg_psum")[i.slot], i.use + 1)
                    act.wait_ge(sem2("agg_sum")[i.slot], i.use)
                    nc.scalar.activation(t256[i.slot][:, 0, :], bank[2 + i.slot][:, D:2 * D], ACT.Copy)\
                        .then_inc(sem2("agg_lo")[i.slot], 1)
            adj_sweep(act, body)

        @block.vector
        def _(dve):
            ch = Chain(dve, "x_stats_chain")
            half = LAST - LAST % 32
            nc.vector.memset(x_all[half:P, T - 1, :], 0.0).then_inc(sem("x_pad_clear"), 1)
            nc.vector.memset(colsum[:, :], 0.0).then_inc(sem("colsum"), 1)
            dve.wait_ge(sem("x_loaded"), 16 * (3 + (1 if LAST % 16 and LAST > 16 else 0)))
            with dve.Fori(0, T) as t:
                nc.vector.bn_stats(stats[:, t, :], x_all[:, t, :]).then_inc(sem("ln_stats"), 1)
            dve.wait_ge(sem("ln_stats"), 1 * T)
            for t in range(T):
                nc.vector.bn_aggr(mv[:, t, :], stats[:, t, :]).then_inc(sem("ln_mv"), 1)
            dve.wait_ge(sem("ln_mv"), 1 * T)
            layernorm_scalars(dve, 0, SCALE)
            dve.wait_ge(sem("w_loaded"), 16 * 5)

            def body(i):
                j = i + 1
                if j.inside(T):
                    dve.wait_ge(sem2("at_used")[j.slot], j.use)
                    dve.wait_ge(sem2("at_stored")[j.slot], 16 * j.use)
                    for c, (t0, n) in enumerate(HCH):
                        s, use = j.ring(NH, c)
                        dve.wait_ge(sem2("tr_psum")[s], use + 1)
                        nc.vector.tensor_copy(at[j.slot][:, t0:t0 + n, :],
                                              bank16(s)[:, 0:n * P].rearrange("p (t c) -> p t c", c=P))\
                            .then_inc(sem2("at_ready")[j.slot], 1)
                        dve.wait_ge(sem2("at_ready")[j.slot], NH * j.use + c + 1)
                        dve.sem_inc(sem2("tr_free")[s], 1)
                    cols = LAST if (j.static and j.t == T - 1) else P
                    dve.wait_ge(sem("colsum"), j.n + 1)
                    nc.vector.tensor_reduce(cs_tmp[:, :], at[j.slot][:, :, 0:cols], AX.X, ALU.add).then_inc(sem("cs_tmp"), 1)
                    dve.wait_ge(sem("cs_tmp"), j.n + 1)
                    nc.vector.tensor_tensor(colsum[:, :], colsum[:, :], cs_tmp[:, :], ALU.add).then_inc(sem("colsum"), 1)
                if i.inside(T):
                    dve.wait_ge(sem2("agg_lo")[i.slot], i.use + 1)
                    dve.wait_ge(sem2("agg_used")[i.slot], i.use)
                    nc.vector.tensor_tensor(xf_sb[i.slot][:, :], bank[2 + i.slot][:, 0:D], t256[i.slot][:, 0, :], ALU.add)\
                        .then_inc(sem2("agg_sum")[i.slot], 1)
                k = i + -1
                if k.inside(T):
                    dve.wait_ge(sem("hw_psum"), k.n + 1)
                    nc.vector.scalar_tensor_tensor(out=xa[:, k.t, :], in0=b_bc, scalar=rowsum[:, k.t, :],
                                                   in1=bank[5][:, 0:D], op0=ALU.mult, op1=ALU.add).then_inc(sem("hw_done"), 1)
            adj_sweep(dve, body)
            _ = ch

        @block.tensor
        def _(pe):
            pe.wait_ge(sem("w_loaded"), 16 * 5)
            pe.wait_ge(sem("consts"), 2)
            pe.wait_ge(sem("const_chain"), 3)
            for k in range(KD):
                last = nc.tensor.transpose(bank[4][0:DA, k * P:(k + 1) * P], w1_sb[:, k, :], ident[:, :])
            last.then_inc(sem("w1t_psum"), 1)
            pe.wait_ge(sem("w1t"), 1)
            for k in range(KD):
                last = nc.tensor.matmul(bank[5][:, k * DA:(k + 1) * DA], w1t_sb[:, k, :], w2_sb, start=True, stop=True)
            last.then_inc(sem("wq_psum"), 1)
            pe.wait_ge(sem("wq"), 1)
            for u in range(2):
                pe.wait_ge(sem2("norm_lo")[u], T // 2)

            def body(i):
                j, k = i + 1, i + -1
                if j.inside(T):
                    pe.wait_ge(sem2("adj16_ready")[j.slot], j.use + 1)
                    for c, (t0, n) in enumerate(HCH):
                        s, use = j.ring(NH, c)
                        pe.wait_ge(sem2("tr_free")[s], use)
                        for t in range(n):
                            last = nc.tensor.transpose(bank16(s)[:, t * P:(t + 1) * P],
                                                       adj16[j.slot][:, (t0 + t) * P:(t0 + t + 1) * P], ident16[:, :])
                        last.then_inc(sem2("tr_psum")[s], 1)
                        if c == NH - 1:
                            pe.wait_ge(sem2("tr_psum")[s], use + 1)
                            pe.sem_inc(sem2("adj16_free")[j.slot], 1)
                if k.inside(T):
                    pe.wait_ge(sem2("agg_sum")[k.slot], k.use + 1)
                    for c in range(KD):
                        last = nc.tensor.transpose(bank[4][:, c * P:(c + 1) * P], xf_sb[k.slot][:, c * P:(c + 1) * P], ident[:, :])
                    last.then_inc(sem("aggT_psum"), 1)
                if i.inside(T):
                    pe.wait_ge(sem2("at_ready")[i.slot], NH * (i.use + 1))
                    pe.wait_ge(sem2("agg_sum")[i.slot], i.use)
                    for t in range(T):
                        last = nc.tensor.matmul(bank[2 + i.slot][:, :], at[i.slot][:, t, :], parts[:, t, :],
                                                start=(t == 0), stop=(t == T - 1))
                    last.then_inc(sem2("agg_psum")[i.slot], 1)
                    pe.wait_ge(sem2("agg_psum")[i.slot], i.use + 1)
                    pe.sem_inc(sem2("at_used")[i.slot], 1)
                if k.inside(T):
                    pe.wait_ge(sem("aggT"), k.n + 1)
                    pe.sem_inc(sem2("agg_used")[k.slot], 1)
                    pe.wait_ge(sem("hw_done"), k.n)
                    for c in range(KD):
                        last = nc.tensor.matmul(bank[5][:, 0:D], zt[:, c, :], w_sb[:, c, :], start=(c == 0), stop=(c == KD - 1))
                    last.then_inc(sem("hw_psum"), 1)
            adj_sweep(pe, body)

    with nc.Block() as block:

        @block.sync
        def _(sp):
            sp.wait_ge(sem("x1"), T)
            sp.dma_start(x1_d, x_all[:, :, :].rearrange("p t d -> p (t d)")).then_inc(sem("x1_stored"), 16)
            for n, u in enumerate((U1, U2, U3)):
                sp.dma_start(u_sb[:, n, :, :], u[0].rearrange("(k p) n -> p k n", p=P)).then_inc(sem("u_loaded"), 16)

            def body(i):
                sp.wait_ge(sem2("q_out")[i.slot], i.use + 1)
                sp.dma_start(q_d[0, dyn(i)], qs[i.slot][0:DA, :]).then_inc(sem2("q_stored")[i.slot], 16)
            sweep(sp, 0, 2, T // 2 - 1, T, body)
            for u in range(2):
                sp.wait_ge(sem2("q_stored")[u], 16 * (T // 2))
            sp.wait_ge(sem("x1_stored"), 16)
            sp.wait_ge(sem("u_loaded"), 48)

        @block.vector
        def _(dve):
            ch = Chain(dve, "mid_chain")
            ch.link(nc.vector.tensor_tensor(colsum[:, T - 1:T], colsum[:, T - 1:T], padone[:, :], ALU.add))
            ch.link(nc.vector.reciprocal(rdeg[:, :, 0], colsum[:, :]))
            ch.link(nc.vector.tensor_scalar(lt[:, :], colsum[:, :], 1.0, 1e-12, ALU.add, ALU.max))
            ch.link(nc.vector.reciprocal(cinv[:, :, 0], lt[:, :]))
            ch.link(nc.vector.tensor_scalar(lt[:, :], rowsum[:, :, 0], 1.0, 1e-12, ALU.add, ALU.max))
            ch.link(nc.vector.reciprocal(rinv[:, :, 0], lt[:, :]))
            ch.link(nc.vector.tensor_tensor(lt[:, :], lt[:, :], cinv[:, :, 0], ALU.mult))
            ch.link(nc.vector.tensor_reduce(ratio[:, :], lt[:, :], AX.X, ALU.max))
            nc.vector.tensor_scalar(ratio[:, :], ratio[:, :], 1.0, None, ALU.max).then_inc(sem("ratio"), 1)
            dve.wait_ge(sem("ratio_all"), 1)
            ch.link(nc.vector.reciprocal(kappa[:, :], ratio_all[:, :]))
            ch.link(nc.vector.tensor_scalar(rinv_s[:, :, 0], rinv[:, :, 0], 1.0 / SCALE, None, ALU.mult))
            ch.link(nc.vector.tensor_scalar(cinv_r[:, :, 0], cinv[:, :, 0], ratio_all[:, :], 1.0 / SCALE, ALU.mult, ALU.mult))
            with dve.Fori(0, T) as t:
                nc.vector.scalar_tensor_tensor(out=x_all[:, t, :], in0=xa[:, t, :], scalar=rdeg[:, t, :],
                                               in1=x_all[:, t, :], op0=ALU.mult, op1=ALU.add).then_inc(sem("x1"), 1)
            dve.wait_ge(sem("x1"), T)
            with dve.Fori(0, T) as t:
                nc.vector.bn_stats(stats[:, t, :], x_all[:, t, :]).then_inc(sem("ln_stats"), 1)
            dve.wait_ge(sem("ln_stats"), 2 * T)
            for t in range(T):
                nc.vector.bn_aggr(mv[:, t, :], stats[:, t, :]).then_inc(sem("ln_mv"), 1)
            dve.wait_ge(sem("ln_mv"), 2 * T)
            layernorm_scalars(dve, 1, 1.0)

            def body(i):
                dve.wait_ge(sem2("norm_hi")[i.slot], i.use + 1 + T // 2)
                nc.vector.scalar_tensor_tensor(out=parts[:, i.t, D:2 * D], in0=xo_sb[i.slot][:, :], scalar=SCALE,
                                               in1=parts[:, i.t, 0:D], op0=ALU.mult, op1=ALU.subtract)\
                    .then_inc(sem2("norm_lo")[i.slot], 1)
                dve.wait_ge(sem2("qk_psum")[i.slot], i.use + 1)
                dve.wait_ge(sem2("q_stored")[i.slot], 16 * i.use)
                nc.vector.tensor_copy(qs[i.slot][0:DA, :], bank[2 + i.slot][0:DA, 0:P]).then_inc(sem2("q_out")[i.slot], 1)
                nc.vector.tensor_copy(keys[0:DA, bass.ds(i.t * P, P)], bank[2 + i.slot][0:DA, P:2 * P])\
                    .then_inc(sem2("qk_done")[i.slot], 1)
            sweep(dve, 0, 2, T // 2 - 1, T, body)

        @block.gpsimd
        def _(pool):
            pool.wait_ge(sem("ratio"), 1)
            nc.gpsimd.partition_all_reduce(ratio_all[:, :], ratio[:, :], P, bass.bass_isa.ReduceOp.max).then_inc(sem("ratio_all"), 1)

            def body(i):
                pool.wait_ge(sem2("normed")[i.slot], i.use + 1 + T // 2)
                nc.gpsimd.tensor_copy(xa[:, i.t, :], xo_sb[i.slot][:, :]).then_inc(sem2("xa_copied")[i.slot], 1)
            sweep(pool, 0, 2, T // 2 - 1, T, body)

        @block.scalar
        def _(act):
            layernorm_sqrt(act, 1)
            act.wait_ge(sem("ln_ready"), 2)

            def body(i):
                act.wait_ge(sem2("xa_copied")[i.slot], i.use)
                act.wait_ge(sem2("norm_lo")[i.slot], i.use + T // 2)
                act.wait_ge(sem2("XT_psum")[i.slot], i.use)
                nc.scalar.activation(xo_sb[i.slot][:, :], x_all[:, i.t, :], ACT.Relu, bias=lb[:, i.t, :], scale=ly[:, i.t, :])\
                    .then_inc(sem2("normed")[i.slot], 1)
                act.wait_ge(sem2("normed")[i.slot], i.use + 1 + T // 2)
                nc.scalar.activation(parts[:, i.t, 0:D], xo_sb[i.slot][:, :], ACT.Copy, scale=SCALE).then_inc(sem2("norm_hi")[i.slot], 1)
                act.wait_ge(sem2("XT_psum")[i.slot], i.use + 1)
                act.wait_ge(sem2("qk_psum")[i.slot], i.use)
                nc.scalar.activation(t256[i.slot][:, 0, :], bank[i.slot][:, 0:D], ACT.Copy).then_inc(sem2("XT")[i.slot], 1)
            sweep(act, 0, 2, T // 2 - 1, T, body)

        @block.tensor
        def _(pe):
            def body(i):
                pe.wait_ge(sem2("normed")[i.slot], i.use + 1 + T // 2)
                pe.wait_ge(sem2("XT")[i.slot], i.use)
                for c in range(KD):
                    last = nc.tensor.transpose(bank[i.slot][:, c * P:(c + 1) * P], xo_sb[i.slot][:, c * P:(c + 1) * P], ident[:, :])
                last.then_inc(sem2("XT_psum")[i.slot], 1)
                pe.wait_ge(sem2("XT")[i.slot], i.use + 1)
                pe.wait_ge(sem2("qk_done")[i.slot], i.use)
                for n, w in enumerate((wq_sb, w3_sb)):
                    for c in range(KD):
                        last = nc.tensor.matmul(bank[2 + i.slot][0:DA, n * P:(n + 1) * P], w[:, c, :],
                                                t256[i.slot][:, 0, c * P:(c + 1) * P], start=(c == 0), stop=(c == KD - 1))
                last.then_inc(sem2("qk_psum")[i.slot], 1)
            sweep(pe, 0, 2, T // 2 - 1, T, body)

    def diffusion_step(s):
        first = s == 0
        row = slice(s * DA, (s + 1) * DA)

        def S(name):
            return sem(f"step_{name}")

        def S2(name):
            return sem2(f"step_{name}")

        def step_sweep(eng, body):
            sweep(eng, -1, 3, (T - 4) // 2, T + 1, body, base=s * T)

        with nc.Block() as block:

            @block.sync
            def _(sp):
                if not first:
                    sp.dma_start(xa[:, :, :], xa_d.rearrange("t p d -> p t d")).then_inc(S("xa_loaded"), 16)
                    for n, u in enumerate((U1, U2, U3)):
                        sp.dma_start(u_sb[:, n, :, :], u[s].rearrange("(k p) n -> p k n", p=P)).then_inc(S("u_loaded"), 16)

                def body(i):
                    j, k = i + 1, i + -1
                    if j.inside(T):
                        sp.wait_ge(S2("at_used")[j.slot], j.use)
                        sp.dma_start(at[j.slot][:, :, :].rearrange("p t c -> p (t c)"), adjT_d[dyn(j)])\
                            .then_inc(S2("at_loaded")[j.slot], 16)
                    if j.inside(T):
                        sp.wait_ge(S2("logits_done")[j.slot], NL * j.use)
                        sp.dma_start(qs[j.slot][row, :], q_d[s, dyn(j)]).then_inc(S2("q_loaded")[j.slot], 16)
                    if not first and i.inside(T):
                        sp.wait_ge(S2("y_done")[i.slot], i.use)
                        sp.dma_start(y_sb[i.slot][:, :], y_d[dyn(i)]).then_inc(S2("y_loaded")[i.slot], 16)
                    if first and k.inside(T):
                        sp.wait_ge(S("qk_done"), k.n + 1)
                        sp.dma_start(q_d[1, dyn(k)], qo[:, :]).then_inc(S("qo_stored"), 16)
                        sp.wait_ge(S2("xo")[k.slot], k.use + 1)
                        sp.dma_start(xa_d[dyn(k)], xo_sb[k.slot][:, :]).then_inc(S2("xo_stored")[k.slot], 16)
                        sp.wait_ge(S2("y_done")[k.slot], k.use + 1)
                        sp.dma_start(y_d[dyn(k)], y_sb[k.slot][:, :]).then_inc(S2("y_stored")[k.slot], 16)
                step_sweep(sp, body)
                if first:
                    sp.wait_ge(S("qo_stored"), 16 * T)
                    for u in range(2):
                        sp.wait_ge(S2("xo_stored")[u], 16 * (T // 2))
                        sp.wait_ge(S2("y_stored")[u], 16 * (T // 2))

            @block.gpsimd
            def _(pool):
                if first:
                    for u in range(2):
                        nc.gpsimd.memset(pb[u][:, N:NP], 0.0).then_inc(S("p_pad"), 1)

                def body(i):
                    j, k = i + 1, i + -1
                    if j.inside(T):
                        pool.wait_ge(S2("at_loaded")[j.slot], 16 * (j.use + 1))
                        nc.gpsimd.tensor_tensor(at[j.slot][:, j.t, :], at[j.slot][:, j.t, :], ident16[:, :], ALU.add)\
                            .then_inc(S2("st_ready")[j.slot], 1)
                    if i.inside(T):
                        for n in range(LOOKS):
                            pool.wait_ge(S("unsettled"), LOOKS * i.n + n + 1)
                            nc.gpsimd.tensor_tensor(pool_tick[:, n:n + 1], padone[:, :], padone[:, :], ALU.add)
                            nc.gpsimd.partition_all_reduce(any_un[:, n:n + 1], unsettled[:, :], P, bass.bass_isa.ReduceOp.max)\
                                .then_inc(S("any_un"), 1)
                    if first and k.inside(T):
                        pool.wait_ge(S2("fb_hi")[k.slot], 3 * (k.use + 1))
                        nc.gpsimd.tensor_tensor(parts_fb[:, k.t, D:2 * D], xf_sb[k.slot][:, :], parts_fb[:, k.t, 0:D], ALU.subtract)\
                            .then_inc(S2("fb_lo")[k.slot], 1)
                        nc.gpsimd.tensor_tensor(parts_fb[:, k.t, 3 * D:4 * D], xk_sb[:, :], parts_fb[:, k.t, 2 * D:3 * D], ALU.subtract)\
                            .then_inc(S2("fb_lo")[k.slot], 1)
                step_sweep(pool, body)

            @block.scalar
            def _(act):
                def body(i):
                    j, k = i + 1, i + -1
                    if k.inside(T):
                        for c, (t0, n) in enumerate(TCH):
                            sl, use = k.ring(NT, c)
                            act.wait_ge(S2("pt_psum")[sl], use + 1)
                            act.wait_ge(S2("pt_used")[sl], use)
                            nc.scalar.activation(pt[sl][:, 0:n * P], bank[2 + sl][:, 0:n * P], ACT.Copy).then_inc(S2("pt")[sl], 1)
                        if first:
                            act.wait_ge(S2("xfb")[k.slot], 2 * (k.use + 1))
                            nc.scalar.activation(parts_fb[:, k.t, 0:D], xf_sb[k.slot][:, :], ACT.Copy).then_inc(S2("fb_hi")[k.slot], 1)
                            act.wait_ge(S2("fb_lo")[1 - k.slot], 2 * (k + 1).use)
                            nc.scalar.activation(xk_sb[:, :], xb_sb[k.slot][:, :], ACT.Copy, scale=kappa[:, :]).then_inc(S2("fb_hi")[k.slot], 1)
                            act.wait_ge(S2("fb_hi")[k.slot], 3 * k.use + 2)
                            nc.scalar.activation(parts_fb[:, k.t, 2 * D:3 * D], xk_sb[:, :], ACT.Copy).then_inc(S2("fb_hi")[k.slot], 1)
                        act.wait_ge(S("fbT_psum"), k.n + 1)
                        act.wait_ge(S("z_psum"), k.n)
                        nc.scalar.activation(zt[:, 0:4, :].rearrange("p k c -> p (k c)"), bank[7][:, :], ACT.Copy,
                                             scale=(1.0 / SCALE if first else 1.0)).then_inc(S("fbT"), 1)
                        act.wait_ge(S("px_psum"), k.n + 1)
                        act.wait_ge(S2("xoT_psum_of")[k.slot], k.use)
                        if first:
                            act.wait_ge(S2("xo_stored")[k.slot], 16 * k.use)
                        nc.scalar.activation(xo_sb[k.slot][:, :], bank[4][:, 0:D], ACT.Copy, scale=rkept[k.slot][:, :])\
                            .then_inc(S2("xo")[k.slot], 1)
                    if j.inside(T):
                        act.wait_ge(S("p_pad"), 2)
                        act.wait_ge(S2("p_used")[j.slot], j.use)
                        for c, (c0, w) in enumerate(LCH):
                            sl, use = j.ring(NL, c)
                            act.wait_ge(S2("logits_psum")[sl], use + 1)
                            nc.scalar.activation(pb[j.slot][:, c0:c0 + w], bank[sl][:, 0:w], ACT.Copy).then_inc(S2("logits_done")[j.slot], 1)
                            act.wait_ge(S2("logits_done")[j.slot], NL * j.use + c + 1)
                            act.sem_inc(S2("logits_free")[sl], 1)
                    if k.inside(T):
                        act.wait_ge(S("xoT_psum"), k.n + 1)
                        nc.scalar.activation(zt[:, 4:6, :].rearrange("p k c -> p (k c)"), bank[7][:, 0:D], ACT.Copy).then_inc(S("xoT"), 1)
                    if i.inside(T):
                        act.wait_ge(S("sx_psum"), i.n + 1)
                        if first:
                            for n, sc in enumerate((rinv, cinv)):
                                nc.scalar.activation(t256[i.slot][:, n, :], bank[5][:, D:2 * D], ACT.Copy, scale=sc[:, i.t, :])\
                                    .then_inc(S2("sx_lo")[i.slot], 1)
                        else:
                            for n, sc in enumerate((rinv_s, cinv_r)):
                                nc.scalar.activation(t256[i.slot][:, n, :], bank[5 + n][:, D:2 * D], ACT.Copy, scale=sc[:, i.t, :])\
                                    .then_inc(S2("sx_lo")[i.slot], 1)
                    if first and k.inside(T):
                        act.wait_ge(S("z_psum"), k.n + 1)
                        r1 = slice(DA, 2 * DA)
                        act.wait_ge(S("qo_stored"), 16 * k.n)
                        nc.scalar.activation(qo[:, :], bank[7][0:DA, D:D + P], ACT.Copy)
                        nc.scalar.activation(keys[r1, bass.ds(k.t * P, P)], bank[7][0:DA, D + P:D + 2 * P], ACT.Copy)\
                            .then_inc(S("qk_done"), 1)
                    if j.inside(T):
                        act.wait_ge(S2("negmax")[j.slot], j.use + 1)
                        nc.scalar.activation(pb[j.slot][:, 0:N], pb[j.slot][:, 0:N], ACT.Exp, bias=negmax[j.slot][:, :],
                                             accum_out=mass[j.slot][:, 0:1]).then_inc(S2("p_ready")[j.slot], 1)
                step_sweep(act, body)

            @block.vector
            def _(dve):
                bisections, interpolations, aim = SEARCH[s]
                K = 2 + bisections
                if first:
                    nc.vector.memset(ones8[:, :], 1.0)
                    for u in range(2):
                        for c, v in ((0, math.exp(-RANGE)), (1, 1.0 + 1e-6), (2, math.exp(-RANGE / 2))):
                            nc.vector.memset(thr[u][:, c:c + 1], v)
                        nc.vector.memset(mass[u][:, 1:2], 0.0)
                    nc.vector.tensor_scalar(pad_target[:, :], padone[:, :], -4.0 * BIG, None, ALU.mult)
                    last = nc.vector.memset(below[:, N:N + 8], 0.0)
                    last.then_inc(S("search_consts"), 1)
                    dve.wait_ge(S("search_consts"), 1)

                def evaluate(ch, p, t, m):
                    ch.link(nc.vector.scalar_tensor_tensor(out=below[:, 0:N], in0=p, scalar=t, in1=p,
                                                           op0=ALU.is_ge, op1=ALU.mult, accum_out=m))

                def narrow(ch, p, last=False):
                    evaluate(ch, p, cur[:, 0:1], cur[:, 1:2])
                    nc.vector.tensor_scalar(m_lo[:, :], cur[:, 1:2], target[:, :], None, ALU.is_ge)
                    ch.link(nc.vector.tensor_scalar(m_hi[:, :], cur[:, 1:2], target[:, :], None, ALU.is_lt), hold=True)
                    nc.vector.copy_predicated(lo[:, :], m_lo[:, :].to_broadcast([P, 2]), cur[:, :])
                    ch.link(nc.vector.copy_predicated(hi[:, :], m_hi[:, :].to_broadcast([P, 2]), cur[:, :]), hold=last)

                def search(i):
                    p, th, ms = pb[i.slot][:, 0:N], thr[i.slot], mass[i.slot]
                    ch = Chain(dve, "step_search", base=i.t * LINKS[s] + sum(LINKS[:s]) * T)
                    dve.wait_ge(S2("p_ready")[i.slot], i.use + 1)
                    if i.static and i.t == T - 1:
                        ch.link(nc.vector.tensor_scalar(target[:, :], ms[:, 0:1], NUCLEUS, pad_target[:, :], ALU.mult, ALU.add))
                    else:
                        ch.link(nc.vector.tensor_scalar(target[:, :], ms[:, 0:1], NUCLEUS, None, ALU.mult))
                    for e in range(bisections):
                        evaluate(ch, p, th[:, 2 + e:3 + e], ms[:, 2 + e:3 + e])
                        if e < bisections - 1:
                            d = RANGE / 2 ** (e + 2)
                            up, down = math.exp(d), math.exp(-d)
                            ch.link(nc.vector.tensor_scalar(factor[:, :], ms[:, 2 + e:3 + e], target[:, :], up - down, ALU.is_ge, ALU.mult))
                            ch.link(nc.vector.scalar_tensor_tensor(out=th[:, 3 + e:4 + e], in0=factor[:, :], scalar=down,
                                                                   in1=th[:, 2 + e:3 + e], op0=ALU.add, op1=ALU.mult))
                    t, m, f, w = th[:, 0:K], ms[:, 0:K], is_lo[:, 0:K], wk[:, 0:K]
                    ch.link(nc.vector.tensor_scalar(f, m, target[:, :], None, ALU.is_ge))
                    ch.link(nc.vector.tensor_tensor(w, f, t, ALU.mult))
                    ch.link(nc.vector.tensor_reduce(lo[:, 0:1], w, AX.X, ALU.max))
                    ch.link(nc.vector.scalar_tensor_tensor(out=w, in0=f, scalar=BIG, in1=t, op0=ALU.mult, op1=ALU.add))
                    ch.link(nc.vector.tensor_reduce(hi[:, 0:1], w, AX.X, ALU.min))
                    ch.link(nc.vector.scalar_tensor_tensor(out=w, in0=f, scalar=-BIG, in1=m, op0=ALU.mult, op1=ALU.add))
                    ch.link(nc.vector.tensor_reduce(hi[:, 1:2], w, AX.X, ALU.max))
                    ch.link(nc.vector.tensor_scalar(w, f, -BIG, BIG, ALU.mult, ALU.add))
                    ch.link(nc.vector.tensor_tensor(w, w, m, ALU.add))
                    ch.link(nc.vector.tensor_reduce(lo[:, 1:2], w, AX.X, ALU.min))
                    for e in range(interpolations):
                        nc.vector.tensor_tensor(frac[:, 0:1], lo[:, 1:2], hi[:, 1:2], ALU.subtract)
                        ch.link(nc.vector.scalar_tensor_tensor(out=frac[:, 1:2], in0=hi[:, 0:1], scalar=-aim, in1=target[:, :],
                                                               op0=ALU.mult, op1=ALU.add))
                        nc.vector.tensor_scalar(frac[:, 1:2], frac[:, 1:2], hi[:, 1:2], 0.0, ALU.subtract, ALU.max)
                        nc.vector.tensor_tensor(frac[:, 2:3], hi[:, 0:1], lo[:, 0:1], ALU.subtract)
                        ch.link(nc.vector.reciprocal(frac[:, 0:1], frac[:, 0:1]))
                        ch.link(nc.vector.scalar_tensor_tensor(out=frac[:, 3:4], in0=frac[:, 1:2], scalar=frac[:, 0:1], in1=frac[:, 2:3],
                                                               op0=ALU.mult, op1=ALU.mult))
                        ch.link(nc.vector.tensor_tensor(cur[:, 0:1], hi[:, 0:1], frac[:, 3:4], ALU.subtract))
                        narrow(ch, p)
                    nc.vector.tensor_copy(run9[:, 0:1], hi[:, 1:2])
                    dve.wait_ge(S("any_un"), LOOKS * i.n)
                    ch.link(nc.vector.scalar_tensor_tensor(out=below[:, 0:N], in0=p, scalar=hi[:, 0:1], in1=p,
                                                           op0=ALU.is_lt, op1=ALU.mult), hold=True)
                    take(ch)
                    dve.sem_inc(S("unsettled"), 1)
                    assert ch.count == LINKS[s], ch.count

                def take(ch):
                    ch.link(nc.vector.max(top8[:, :], below[:, :]))
                    ch.link(nc.vector.tensor_tensor_scan(run9[:, 1:9], ones8[:, :], top8[:, :], run9[:, 0:1], ALU.mult, ALU.add))
                    ch.link(nc.vector.scalar_tensor_tensor(out=take8[:, :], in0=run9[:, 0:8], scalar=target[:, :], in1=top8[:, :],
                                                           op0=ALU.is_lt, op1=ALU.mult))
                    ch.link(nc.vector.tensor_tensor_scan(run8[:, :], ones8[:, :], take8[:, :], run9[:, 0:1], ALU.mult, ALU.add))
                    nc.vector.tensor_copy(run9[:, 0:1], run8[:, 7:8])
                    ch.link(nc.vector.tensor_scalar(unsettled[:, :], run8[:, 7:8], target[:, :], None, ALU.is_lt), hold=True)
                    ch.link(nc.vector.match_replace(below[:, :], take8[:, :], below[:, :], 0.0), hold=True)

                def look(i, n):
                    dve.wait_ge(S("any_un"), LOOKS * i.n + n)
                    nc.vector.memset(tick[:, n:n + 1], 0.0)
                    return dve.value_load(any_un[0:1, n - 1:n].bitcast(i32))

                def settle(i, level=0):
                    links = TAKE * ROUNDS[level]
                    done = S(f"settle_{level}")
                    with dve.If(look(i, level + 1) > 0):
                        with dve.Fori(0, ROUNDS[level]) as g:
                            take(Chain(dve, f"step_settle_{level}", base=links * i.n + TAKE * g))
                        if level + 1 < LOOKS:
                            dve.sem_inc(S("unsettled"), 1)
                            settle(i, level + 1)
                    with dve.Else():
                        dve.sem_inc(done, links)
                        for deeper in range(level + 1, LOOKS):
                            dve.sem_inc(S("unsettled"), 1)
                            dve.sem_inc(S(f"settle_{deeper}"), TAKE * ROUNDS[deeper])

                def body(i):
                    j, k = i + 1, i + -1
                    if i.inside(T):
                        search(i)
                    if j.inside(T):
                        dve.wait_ge(S2("logits_done")[j.slot], NL * (j.use + 1))
                        nc.vector.tensor_reduce(negmax[j.slot][:, :], pb[j.slot][:, 0:N], AX.X, ALU.max, negate=True)\
                            .then_inc(S2("negmax")[j.slot], 1)
                    if i.inside(T):
                        settle(i)
                        dve.wait_ge(S2("xo")[i.slot], i.use)
                        nc.vector.reciprocal(rkept[i.slot][:, :], run9[:, 0:1])
                        p = pb[i.slot][:, 0:N]
                        nc.vector.tensor_tensor(p, p, below[:, 0:N], ALU.subtract).then_inc(S2("masked")[i.slot], 1)
                        dve.wait_ge(S2("sx_lo")[i.slot], 2 * (i.use + 1))
                        if first:
                            dve.wait_ge(S2("fb_lo")[i.slot], 2 * i.use)
                        dve.wait_ge(S2("fbT_psum_of")[i.slot], i.use)
                        for n, (dst, sc) in enumerate(((xf_sb, rinv if first else rinv_s), (xb_sb, cinv if first else cinv_r))):
                            nc.vector.scalar_tensor_tensor(out=dst[i.slot][:, :], in0=bank[5 if first else 5 + n][:, 0:D],
                                                           scalar=sc[:, i.t, :], in1=t256[i.slot][:, n, :],
                                                           op0=ALU.mult, op1=ALU.add).then_inc(S2("xfb")[i.slot], 1)
                    if k.inside(T):
                        dve.wait_ge(S("z_psum"), k.n + 1)
                        if first:
                            dve.wait_ge(S("qk_done"), k.n + 1)
                            dve.wait_ge(S2("y_stored")[k.slot], 16 * k.use)
                            nc.vector.tensor_tensor(y_sb[k.slot][:, :], bank[7][:, 0:D], xa[:, k.t, :], ALU.add).then_inc(S2("y_done")[k.slot], 1)
                        else:
                            dve.wait_ge(S2("y_loaded")[k.slot], 16 * (k.use_here + 1))
                            nc.vector.tensor_tensor(yall[:, k.t, :], bank[7][:, 0:D], y_sb[k.slot][:, :], ALU.add).then_inc(S2("y_done")[k.slot], 1)
                step_sweep(dve, body)

            @block.tensor
            def _(pe):
                if not first:
                    pe.wait_ge(S("xa_loaded"), 16)
                    pe.wait_ge(S("u_loaded"), 48)

                def body(i):
                    j, k = i + 1, i + -1
                    if k.inside(T):
                        pe.wait_ge(S2("masked")[k.slot], k.use + 1)
                        pe.wait_ge(S("p_pad"), 2)

                        def transposes(c):
                            t0, n = TCH[c]
                            sl, use = k.ring(NT, c)
                            pe.wait_ge(S2("pt")[sl], use)
                            for t in range(n):
                                last = nc.tensor.transpose(bank[2 + sl][:, t * P:(t + 1) * P],
                                                           pb[k.slot][:, (t0 + t) * P:(t0 + t + 1) * P], ident[:, :])
                            last.then_inc(S2("pt_psum")[sl], 1)

                        def product(c):
                            t0, n = TCH[c]
                            sl, use = k.ring(NT, c)
                            pe.wait_ge(S2("pt")[sl], use + 1)
                            for t in range(n):
                                last = nc.tensor.matmul(bank[4][:, 0:D], pt[sl][:, t * P:(t + 1) * P], xa[:, t0 + t, :],
                                                        start=(t0 + t == 0), stop=(t0 + t == T - 1))
                            last.then_inc(S2("pt_used")[sl], 1)

                        transposes(0)
                        pe.wait_ge(S2("xo")[1 - k.slot], (k + 1).use)
                        for c in range(NT):
                            if c + 1 < NT:
                                transposes(c + 1)
                            product(c)
                        sl, use = k.ring(NT, NT - 1)
                        pe.wait_ge(S2("pt_used")[sl], use + 1)
                        pe.sem_inc(S2("p_used")[k.slot], 1)
                        pe.sem_inc(S("px_psum"), 1)
                        pe.wait_ge(S2("xfb")[k.slot], 2 * (k.use + 1))
                        pe.wait_ge(S2("y_done")[1 - k.slot], (k + 1).use)
                        if first:
                            pe.wait_ge(S("qk_done"), k.n)
                        for n, src in enumerate((xf_sb, xb_sb)):
                            for c in range(KD):
                                q = n * KD + c
                                last = nc.tensor.transpose(bank[7][:, q * P:(q + 1) * P], src[k.slot][:, c * P:(c + 1) * P], ident[:, :])
                        last.then_inc(S("fbT_psum"), 1)
                        pe.wait_ge(S("fbT_psum"), k.n + 1)
                        pe.sem_inc(S2("fbT_psum_of")[k.slot], 1)
                    if j.inside(T):
                        pe.wait_ge(S2("q_loaded")[j.slot], 16 * (j.use + 1))
                        for c, (c0, w) in enumerate(LCH):
                            sl, use = j.ring(NL, c)
                            pe.wait_ge(S2("logits_free")[sl], use)
                            nc.tensor.matmul(bank[sl][:, 0:w], qs[j.slot][row, :], keys[row, c0:c0 + w], start=True, stop=True)\
                                .then_inc(S2("logits_psum")[sl], 1)
                    if k.inside(T):
                        pe.wait_ge(S2("xo")[k.slot], k.use + 1)
                        pe.wait_ge(S("fbT"), k.n + 1)
                        for c in range(KD):
                            last = nc.tensor.transpose(bank[7][:, c * P:(c + 1) * P], xo_sb[k.slot][:, c * P:(c + 1) * P], ident[:, :])
                        last.then_inc(S("xoT_psum"), 1)
                        pe.wait_ge(S("xoT_psum"), k.n + 1)
                        pe.sem_inc(S2("xoT_psum_of")[k.slot], 1)
                    if i.inside(T):
                        pe.wait_ge(S2("st_ready")[i.slot], i.use + 1)
                        pe.wait_ge(S2("xfb")[1 - i.slot], 2 * (i + 1).use)
                        for n in range(1 if first else 2):
                            for t in range(T):
                                mov = parts[:, t, :] if first else parts_fb[:, t, n * 2 * D:(n + 1) * 2 * D]
                                last = nc.tensor.matmul(bank[5 + n][:, :], at[i.slot][:, t, :], mov, start=(t == 0), stop=(t == T - 1))
                        last.then_inc(S("sx_psum"), 1)
                        pe.wait_ge(S("sx_psum"), i.n + 1)
                        pe.sem_inc(S2("at_used")[i.slot], 1)
                    if k.inside(T):
                        pe.wait_ge(S("xoT"), k.n + 1)
                        for q in range(6):
                            last = nc.tensor.matmul(bank[7][:, 0:D], zt[:, q, :], u_sb[:, q // KD, q % KD, :],
                                                    start=(q == 0), stop=(q == 5))
                        if first:
                            for n, w in enumerate((wq_sb, w3_sb)):
                                for c in range(KD):
                                    last = nc.tensor.matmul(bank[7][0:DA, D + n * P:D + (n + 1) * P], w[:, c, :], zt[:, 4 + c, :],
                                                            start=(c == 0), stop=(c == KD - 1))
                        last.then_inc(S("z_psum"), 1)
                step_sweep(pe, body)

    diffusion_step(0)
    diffusion_step(1)

    with nc.Block() as block:

        @block.sync
        def _(sp):
            sp.dma_start(xa[:, :, :].rearrange("p t d -> p (t d)"), x1_d).then_inc(sem("x1_loaded"), 16)
            sp.dma_start(gamma_bc, bc(gamma)).then_inc(sem("x1_loaded"), 16)
            sp.dma_start(beta_bc, bc(beta)).then_inc(sem("x1_loaded"), 16)

            def body(i):
                sp.wait_ge(sem2("o_done")[i.slot], i.use + 1)
                sp.dma_start(out_t[dyn(i)], xo_sb[i.slot][:, :]).then_inc(sem2("o_stored")[i.slot], 16)
            out_t = out[0:(T - 1) * P, :].rearrange("(t p) n -> t p n", p=P)
            sweep(sp, 0, 2, (T - 1) // 2 - 1, T - 1, body)
            i = Idx(0, T - 1)
            sp.wait_ge(sem2("o_done")[i.slot], i.use + 1)
            even = LAST - LAST % 16
            for r0, r1 in ((0, even), (even, LAST)):
                if r1 > r0:
                    sp.dma_start(out[(T - 1) * P + r0:(T - 1) * P + r1, :], xo_sb[i.slot][r0:r1, :]).then_inc(sem("o_last_stored"), 16)
            sp.wait_ge(sem("o_last_stored"), 16 * (2 if LAST % 16 and LAST > 16 else 1))
            sp.wait_ge(sem2("o_stored")[0], 16 * (T // 2))
            sp.wait_ge(sem2("o_stored")[1], 16 * (T // 2 - 1))

        @block.scalar
        def _(act):
            layernorm_sqrt(act, 2)
            act.wait_ge(sem("ln_ready"), 3)

            def body(i):
                act.wait_ge(sem2("o_done")[i.slot], i.use)
                nc.scalar.activation(xf_sb[i.slot][:, :], yall[:, i.t, :], ACT.Identity, bias=lb[:, i.t, :], scale=ly[:, i.t, :])\
                    .then_inc(sem2("normed")[i.slot], 1)
            sweep(act, 0, 2, T // 2 - 1, T, body)

        @block.vector
        def _(dve):
            with dve.Fori(0, T) as t:
                nc.vector.bn_stats(stats[:, t, :], yall[:, t, :]).then_inc(sem("ln_stats"), 1)
            dve.wait_ge(sem("ln_stats"), 3 * T)
            for t in range(T):
                nc.vector.bn_aggr(mv[:, t, :], stats[:, t, :]).then_inc(sem("ln_mv"), 1)
            dve.wait_ge(sem("ln_mv"), 3 * T)
            layernorm_scalars(dve, 2, 1.0)
            dve.wait_ge(sem("x1_loaded"), 48)

            def body(i):
                ch = Chain(dve, "out_chain", base=2 * i.n)
                dve.wait_ge(sem2("normed")[i.slot], i.use + 1 + T)
                ch.link(nc.vector.tensor_tensor(xb_sb[i.slot][:, :], xf_sb[i.slot][:, :], gamma_bc, ALU.mult))
                ch.link(nc.vector.tensor_tensor(xb_sb[i.slot][:, :], xb_sb[i.slot][:, :], beta_bc, ALU.add))
                dve.wait_ge(sem2("o_stored")[i.slot], 16 * i.use)
                nc.vector.tensor_tensor(xo_sb[i.slot][:, :], xb_sb[i.slot][:, :], xa[:, i.t, :], ALU.add).then_inc(sem2("o_done")[i.slot], 1)
            sweep(dve, 0, 2, T // 2 - 1, T, body)


_INS = ["x", "adj", "L0_gnn_W", "L0_gnn_b", "L1_gnn_W1", "L1_gnn_W2", "L1_gnn_W3",
        "L1_gnn_U1", "L1_gnn_U2", "L1_gnn_U3", "L1_gnn_gamma", "L1_gnn_beta"]


def kernel(**inputs):
    import numpy as _np
    import concourse.bacc as _bacc
    from concourse import mybir as _mybir
    from concourse.bass_utils import run_bass_kernel_spmd as _run

    nc = _bacc.Bacc("TRN2", target_bir_lowering=False, num_devices=1)
    arrays, args = {}, []
    for name in _INS:
        a = _np.ascontiguousarray(inputs[name])
        arrays[f"in_{name}_dram"] = a
        args.append(nc.dram_tensor(f"in_{name}_dram", a.shape, _mybir.dt.from_np(a.dtype), kind="ExternalInput").ap())
    o = nc.dram_tensor("out_0_dram", inputs["x"].shape, _mybir.dt.float32, kind="ExternalOutput").ap()
    gnn_program(nc, *args, o)
    r = _run(nc, [arrays], core_ids=[0])
    return r.results[0]["out_0_dram"]
```

```python
import math

import numpy as np
import concourse.bass as bass
from concourse import mybir


class Idx:

    def __init__(self, g, off, base=0):
        self.g, self.off, self.base = g, off, base
        self.static = isinstance(g, int)
        self.t = 2 * g + off
        self.n = 2 * g + (off + base)
        self.slot = off % 2
        self.use = g + (off + base) // 2
        self.use_here = g + off // 2

    def __add__(self, d):
        return Idx(self.g, self.off + d, self.base)

    def inside(self, tiles):
        return not self.static or 0 <= self.t < tiles

    def ring(self, per, c):
        s = per * (self.off + self.base) + c
        return s % 2, per * self.g + s // 2


def gnn_program(nc, x, adj, W, b, W1, W2, W3, U1, U2, U3, gamma, beta, out):
    f32, f16, i32 = mybir.dt.float32, mybir.dt.float16, mybir.dt.int32
    ALU, ACT, AX = mybir.AluOpType, mybir.ActivationFunctionType, mybir.AxisListType

    P = 128
    N, D = x.shape
    DA = W2.shape[0]
    KD = D // P
    T = -(-N // P)
    NP = T * P
    LAST = N - (T - 1) * P
    EPS = 1e-5
    SCALE = 1024.0
    NUCLEUS = 0.9
    CW = 512
    LCH = [(c, min(CW, N - c)) for c in range(0, N, CW)]
    TCH = [(c, min(7, T - c)) for c in range(0, T, 7)]
    HCH = [(c, min(8, T - c)) for c in range(0, T, 8)]
    NL, NT, NH = len(LCH), len(TCH), len(HCH)
    RANGE = math.log(N / (1 - NUCLEUS)) + 0.01
    SEARCH = ((5, 2, 2.5), (7, 3, 5.0))
    KMAX = 2 + max(b for b, _, _ in SEARCH)
    ACT_BISECTIONS = (3, 5)
    MOST = max(ACT_BISECTIONS)
    ACT_LINKS = [9 * b for b in ACT_BISECTIONS]
    FEW_ROUNDS = 2
    ALL_ROUNDS = -(-N // 8)
    LOOKS = 3
    BIG = 2.0 ** 40
    TAKE = 6
    TIES, FEW = 8, 2 + TAKE * FEW_ROUNDS
    LINKS = [1 + 3 * (b - AB) - 2 + 10 + 7 * n + 14 for (b, n, _), AB in zip(SEARCH, ACT_BISECTIONS)]

    adjT_d = nc.dram_tensor("adjT_d", [T, P, T * P], f16, kind="Internal").ap()
    q_d = nc.dram_tensor("q_d", [2, T, DA, P], f32, kind="Internal").ap()
    x1_d = nc.dram_tensor("x1_d", [P, T * D], f32, kind="Internal").ap()
    y_d = nc.dram_tensor("y_d", [T, P, D], f32, kind="Internal").ap()
    fb_d = nc.dram_tensor("fb_d", [T, P, 4 * D], f16, kind="Internal").ap()
    xa_d = nc.dram_tensor("xa_d", [T, P, D], f32, kind="Internal").ap()

    def sb(name, shape, dt):
        return nc.alloc_sbuf_tensor(name, shape, dt)

    sem_names = {}

    def sem(name):
        if name not in sem_names:
            sem_names[name] = nc.alloc_semaphore(name)
        return sem_names[name]

    def sem2(name):
        return [sem(f"{name}_{u}") for u in range(2)]


    region = sb("region", [P, T * 2 * D], f32)
    xa = sb("xa", [P, T, D], f32)
    keys = sb("keys", [P, NP], f32)
    at = [sb(f"at{u}", [P, T, P], f16) for u in range(2)]
    pb_all = sb("pb_all", [P, 2 * NP], f32)
    pb = [pb_all[:, u * NP:(u + 1) * NP] for u in range(2)]
    below = sb("below", [P, N + 8], f32)
    kept_p = sb("kept_p", [P, NP], f32)
    junk_v = sb("junk_v", [P, NP], f16)
    junk_a = sb("junk_a", [P, NP], f16)
    fb_sb = sb("fb_sb", [P, 4 * D], f16)
    pt = [sb(f"pt{u}", [P, 7 * P], f32) for u in range(2)]
    parts = region[:, 0:T * D].bitcast(f16).rearrange("p (t c) -> p t c", c=2 * D)
    yall = region[:, 0:T * D].rearrange("p (t d) -> p t d", d=D)
    parts_fb = region[:, :].bitcast(f16).rearrange("p (t c) -> p t c", c=4 * D)
    adj_in = [region[:, (2 + u) * NP:(3 + u) * NP] for u in range(2)]
    adj16 = [junk_v[:, :], junk_a[:, :]]
    x_all = pb_all[:, :].rearrange("p (t d) -> p t d", d=D)

    ident = sb("ident", [P, P], f32)
    ident16 = sb("ident16", [P, P], f16)
    padone = sb("padone", [P, 1], f32)
    early = below[:, :]
    w_sb = early[:, 0:KD * D].rearrange("p (k d) -> p k d", d=D)
    b_bc = early[:, KD * D:(KD + 1) * D]
    e0 = (KD + 1) * D
    w1_sb = early[:, e0:e0 + KD * DA].rearrange("p (k d) -> p k d", d=DA)
    w1t_sb = early[0:DA, e0 + KD * DA:e0 + KD * (DA + P)].rearrange("p (k d) -> p k d", d=P)
    w2_sb = early[0:DA, e0 + KD * (DA + P):e0 + KD * (DA + P) + DA]
    gamma_bc = keys[:, 0:D]
    beta_bc = keys[:, D:2 * D]
    wq_sb = sb("wq_sb", [P, KD, DA], f32)
    w3_sb = sb("w3_sb", [P, KD, DA], f32)
    u_sb = sb("u_sb", [P, 3, KD, D], f32)
    stats = sb("stats", [P, T, 6], f32)
    mv = sb("mv", [P, T, 2], f32)
    ve = sb("ve", [P, T], f32)
    sd = sb("sd", [P, T], f32)
    lt = sb("lt", [P, T], f32)
    ly = sb("ly", [P, T, 1], f32)
    lb = sb("lb", [P, T, 1], f32)
    rowsum = sb("rowsum", [P, T, 1], f32)
    colsum = sb("colsum", [P, T], f32)
    cs_tmp = sb("cs_tmp", [P, T], f32)
    rdeg = sb("rdeg", [P, T, 1], f32)
    rinv = sb("rinv", [P, T, 1], f32)
    cinv = sb("cinv", [P, T, 1], f32)
    cinv_r = sb("cinv_r", [P, T, 1], f32)
    rinv_s = sb("rinv_s", [P, T, 1], f32)
    ratio = sb("ratio", [P, 1], f32)
    ratio_all = sb("ratio_all", [P, 1], f32)
    kappa = sb("kappa", [P, 1], f32)
    t256 = [sb(f"t256_{u}", [P, 2, D], f32) for u in range(2)]
    xf_sb = [sb(f"xf_sb{u}", [P, D], f32) for u in range(2)]
    xb_sb = [sb(f"xb_sb{u}", [P, D], f32) for u in range(2)]
    xo_sb = [sb(f"xo_sb{u}", [P, D], f32) for u in range(2)]
    xk_sb = sb("xk_sb", [P, D], f32)
    zt = sb("zt", [P, 6, P], f32)
    y_sb = [sb(f"y_sb{u}", [P, D], f32) for u in range(2)]
    qs = [sb(f"qs{u}", [P, P], f32) for u in range(2)]
    qo = sb("qo", [DA, P], f32)
    negmax = [sb(f"negmax{u}", [P, 1], f32) for u in range(2)]
    thr = [sb(f"thr{u}", [P, KMAX], f32) for u in range(2)]
    mass = [sb(f"mass{u}", [P, KMAX], f32) for u in range(2)]
    target = sb("target", [P, 1], f32)
    nucleus_pad = sb("nucleus_pad", [P, 1], f32)
    factor = sb("factor", [P, 1], f32)
    is_lo = sb("is_lo", [P, KMAX], f32)
    wk = sb("wk", [P, KMAX], f32)
    lo = sb("lo", [P, 2], f32)
    hi = sb("hi", [P, 2], f32)
    cur = sb("cur", [P, 2], f32)
    m_lo = sb("m_lo", [P, 1], i32)
    m_hi = sb("m_hi", [P, 1], i32)
    frac = sb("frac", [P, 4], f32)
    ones8 = sb("ones8", [P, 8], f32)
    top8 = sb("top8", [P, 8], f32)
    take8 = sb("take8", [P, 8], f32)
    run9 = sb("run9", [P, 9], f32)
    run8 = sb("run8", [P, 8], f32)
    took = sb("took", [P, 1], f32)
    left = sb("left", [P, 8], f32)
    left_max = sb("left_max", [P, 1], f32)
    tied = sb("tied", [P, 1], f32)
    edges = sb("edges", [P, 9], f32)
    edge = sb("edge", [P, 1], f32)
    edge_mass = sb("edge_mass", [P, 1], f32)
    tie = sb("tie", [P, 4], f32)
    below_sum = sb("below_sum", [P, 1], f32)
    log_t = [sb(f"log_t{u}", [P, MOST + 1], f32) for u in range(2)]
    minus_t = [sb(f"minus_t{u}", [P, MOST], f32) for u in range(2)]
    n_t = [sb(f"n_t{u}", [P, MOST], f32) for u in range(2)]
    over = [sb(f"over{u}", [P, 5], f32) for u in range(2)]
    unsettled = sb("unsettled", [P, 1], f32)
    any_un = sb("any_un", [P, LOOKS], f32)
    tick = sb("tick", [1, 1 + LOOKS], f32)
    pool_tick = sb("pool_tick", [P, LOOKS], f32)
    rkept = [sb(f"rkept{u}", [P, 1], f32) for u in range(2)]

    pairs = [nc.alloc_psum_tensor(f"banks{2 * i}", [P, 2 * CW], f32) for i in range(4)]
    bank = [pairs[i // 2][:, i % 2 * CW:(i % 2 + 1) * CW] for i in range(8)]
    pt_ps = [pairs[1], pairs[0]]

    def bank16(i):
        return bank[i].bitcast(f16)

    class Chain:

        def __init__(self, eng, name, base=0):
            self.eng, self.sem, self.base, self.count = eng, sem(name), base, 0

        def link(self, ins, hold=False):
            self.count += 1
            ins.then_inc(self.sem, 1)
            self.eng.wait_ge(self.sem, self.base + self.count)
            if hold:
                nc.vector.memset(tick[:, 0:1], 0.0)

    def layernorm_scalars(dve, call, scale):
        ch = Chain(dve, "ln_chain", base=7 * call)
        ch.link(nc.vector.tensor_scalar(ve[:, :], mv[:, :, 1], EPS, None, ALU.add))
        ch.eng.sem_inc(sem("ln_var"), 1)
        dve.wait_ge(sem("ln_sqrt"), call + 1)
        ch.link(nc.vector.reciprocal(sd[:, :], sd[:, :]))
        ch.link(nc.vector.tensor_tensor(lt[:, :], sd[:, :], sd[:, :], ALU.mult))
        ch.link(nc.vector.tensor_tensor(lt[:, :], lt[:, :], ve[:, :], ALU.mult))
        ch.link(nc.vector.tensor_scalar(lt[:, :], lt[:, :], -0.5 * scale, 1.5 * scale, ALU.mult, ALU.add))
        ch.link(nc.vector.tensor_tensor(ly[:, :, 0], sd[:, :], lt[:, :], ALU.mult))
        ch.link(nc.vector.tensor_tensor(lt[:, :], mv[:, :, 0], ly[:, :, 0], ALU.mult))
        nc.vector.tensor_scalar(lb[:, :, 0], lt[:, :], -1.0, None, ALU.mult).then_inc(sem("ln_ready"), 1)

    def layernorm_sqrt(act, call):
        act.wait_ge(sem("ln_var"), call + 1)
        nc.scalar.activation(sd[:, :], ve[:, :], ACT.Sqrt).then_inc(sem("ln_sqrt"), 1)

    def sweep(eng, first, loop_from, pairs, last, body, base=0):
        for i in range(first, loop_from):
            body(Idx(0, i, base))
        with eng.Fori(0, pairs) as g:
            for u in range(2):
                body(Idx(g, loop_from + u, base))
        for i in range(loop_from + 2 * pairs, last):
            body(Idx(0, i, base))

    def dyn(i):
        return i.t

    def adj_sweep(eng, body):
        sweep(eng, -2, 3, (T - 6) // 2, T + 1, body)

    def bc(v):
        return v.partition_broadcast(P)

    XH = T // 2
    with nc.Block() as block:

        @block.sync
        def _(sp):
            sp.wait_ge(sem("x_pad_clear"), 1)
            sp.dma_start(x_all[:, 0:XH, :], x[0:XH * P, :].rearrange("(t p) d -> p t d", p=P)).then_inc(sem("x_loaded"), 16)
            sp.dma_start(x_all[:, XH:T - 1, :], x[XH * P:(T - 1) * P, :].rearrange("(t p) d -> p t d", p=P)).then_inc(sem("x_loaded"), 16)
            even = LAST - LAST % 16
            for r0, r1 in ((0, even), (even, LAST)):
                if r1 > r0:
                    sp.dma_start(x_all[r0:r1, T - 1, :], x[(T - 1) * P + r0:(T - 1) * P + r1, :]).then_inc(sem("x_loaded"), 16)
            sp.dma_start(w_sb[:, :, :], W.rearrange("(k p) n -> p k n", p=P)).then_inc(sem("w_loaded"), 16)
            sp.dma_start(b_bc, bc(b)).then_inc(sem("w_loaded"), 16)
            sp.dma_start(w1_sb[:, :, :], W1.rearrange("(k p) n -> p k n", p=P)).then_inc(sem("w_loaded"), 16)
            sp.dma_start(w3_sb[:, :, :], W3.rearrange("(k p) n -> p k n", p=P)).then_inc(sem("w_loaded"), 16)
            sp.dma_start(w2_sb, W2).then_inc(sem("w_loaded"), 16)

            def body(i):
                j = i + 2
                if j.inside(T):
                    sp.wait_ge(sem2("adj_in_free")[j.slot], j.use)
                    if j.static and j.t == T - 1:
                        for r0, r1 in ((0, even), (even, LAST)):
                            if r1 > r0:
                                sp.dma_start(adj_in[j.slot][r0:r1, 0:N], adj[(T - 1) * P + r0:(T - 1) * P + r1, :])\
                                    .then_inc(sem("adj_last_loaded"), 16)
                    else:
                        sp.dma_start(adj_in[j.slot][:, 0:N], adj_t[dyn(j)]).then_inc(sem2("adj_loaded")[j.slot], 16)
                if i.inside(T):
                    sp.wait_ge(sem2("at_ready")[i.slot], NH * (i.use + 1))
                    sp.dma_start(adjT_d[dyn(i)], at[i.slot][:, :, :].rearrange("p t c -> p (t c)"))\
                        .then_inc(sem2("at_stored")[i.slot], 16)

            adj_t = adj[0:(T - 1) * P, :].rearrange("(t p) n -> t p n", p=P)
            adj_sweep(sp, body)
            for u in range(2):
                sp.wait_ge(sem2("at_stored")[u], 16 * (T // 2))

        @block.gpsimd
        def _(pool):
            nc.gpsimd.memset(ident[:, :], 0.0).then_inc(sem("const_chain"), 1)
            nc.gpsimd.memset(padone[:, :], 1.0).then_inc(sem("const_chain"), 1)
            for u in range(2):
                nc.gpsimd.memset(adj_in[u][:, N:NP], 0.0).then_inc(sem("adj_pad"), 1)
            pool.wait_ge(sem("const_chain"), 2)
            nc.gpsimd.affine_select(out=ident[:, :], in_=ident[:, :], compare_op=ALU.not_equal, fill=1.0, base=0,
                                    pattern=[[-1, P]], channel_multiplier=1).then_inc(sem("const_chain"), 1)
            nc.gpsimd.affine_select(out=padone[:, :], in_=padone[:, :], compare_op=ALU.is_ge, fill=0.0, base=-LAST,
                                    pattern=[[0, 1]], channel_multiplier=1).then_inc(sem("consts"), 1)
            pool.wait_ge(sem("const_chain"), 3)
            nc.gpsimd.tensor_copy(ident16[:, :], ident[:, :]).then_inc(sem("consts"), 1)

            def low(i):
                pool.wait_ge(sem2("norm_hi")[i.slot], i.use + 1)
                nc.gpsimd.tensor_tensor(parts[:, i.t, D:2 * D], xo_sb[i.slot][:, :], parts[:, i.t, 0:D], ALU.subtract)\
                    .then_inc(sem2("norm_lo")[i.slot], 1)
            sweep(pool, 0, 2, T // 2 - 1, T, low)

        @block.scalar
        def _(act):
            layernorm_sqrt(act, 0)
            act.wait_ge(sem("ln_ready"), 1)

            def split(i):
                act.wait_ge(sem2("norm_lo")[i.slot], i.use)
                nc.scalar.activation(xo_sb[i.slot][:, :], x_all[:, i.t, :], ACT.Relu, bias=lb[:, i.t, :], scale=ly[:, i.t, :])\
                    .then_inc(sem2("normed")[i.slot], 1)
                act.wait_ge(sem2("normed")[i.slot], i.use + 1)
                nc.scalar.activation(parts[:, i.t, 0:D], xo_sb[i.slot][:, :], ACT.Copy).then_inc(sem2("norm_hi")[i.slot], 1)
            sweep(act, 0, 2, T // 2 - 1, T, split)
            act.wait_ge(sem("w1t_psum"), 1)
            nc.scalar.activation(w1t_sb[:, :, :].rearrange("p k c -> p (k c)"), bank[4][0:DA, 0:KD * P], ACT.Copy).then_inc(sem("w1t"), 1)
            act.wait_ge(sem("wq_psum"), 1)
            nc.scalar.activation(wq_sb[:, :, :].rearrange("p k c -> p (k c)"), bank[5][:, 0:KD * DA], ACT.Copy).then_inc(sem("wq"), 1)
            act.wait_ge(sem("adj_pad"), 2)

            def body(i):
                j = i + 2
                if j.inside(T):
                    if j.static and j.t == T - 1:
                        act.wait_ge(sem("adj_last_loaded"), 16 * (2 if LAST % 16 and LAST > 16 else 1))
                    else:
                        act.wait_ge(sem2("adj_loaded")[j.slot], 16 * (j.use + 1))
                    act.wait_ge(sem2("adj16_free")[j.slot], j.use)
                    nc.scalar.activation(adj16[j.slot], adj_in[j.slot], ACT.Copy, accum_out=rowsum[:, j.t, :])\
                        .then_inc(sem2("adj16_ready")[j.slot], 1)
                    act.wait_ge(sem2("adj16_ready")[j.slot], j.use + 1)
                    act.sem_inc(sem2("adj_in_free")[j.slot], 1)
                k = i + -1
                if k.inside(T):
                    act.wait_ge(sem("aggT_psum"), k.n + 1)
                    nc.scalar.activation(zt[:, 0:KD, :], bank[4][:, 0:KD * P].rearrange("p (k c) -> p k c", c=P), ACT.Copy,
                                         scale=1.0 / SCALE).then_inc(sem("aggT"), 1)
                if i.inside(T):
                    act.wait_ge(sem2("agg_psum")[i.slot], i.use + 1)
                    act.wait_ge(sem2("agg_sum")[i.slot], i.use)
                    nc.scalar.activation(t256[i.slot][:, 0, :], bank[2 + i.slot][:, D:2 * D], ACT.Copy)\
                        .then_inc(sem2("agg_lo")[i.slot], 1)
            adj_sweep(act, body)

        @block.vector
        def _(dve):
            ch = Chain(dve, "x_stats_chain")
            half = LAST - LAST % 32
            nc.vector.memset(x_all[half:P, T - 1, :], 0.0).then_inc(sem("x_pad_clear"), 1)
            nc.vector.memset(colsum[:, :], 0.0).then_inc(sem("colsum"), 1)
            dve.wait_ge(sem("x_loaded"), 16 * (3 + (1 if LAST % 16 and LAST > 16 else 0)))
            with dve.Fori(0, T // 4) as g:
                for u in range(4):
                    nc.vector.bn_stats(stats[:, 4 * g + u, :], x_all[:, 4 * g + u, :]).then_inc(sem("ln_stats"), 1)
            for t in range(T // 4 * 4, T):
                nc.vector.bn_stats(stats[:, t, :], x_all[:, t, :]).then_inc(sem("ln_stats"), 1)
            dve.wait_ge(sem("ln_stats"), 1 * T)
            for t in range(T):
                nc.vector.bn_aggr(mv[:, t, :], stats[:, t, :]).then_inc(sem("ln_mv"), 1)
            dve.wait_ge(sem("ln_mv"), 1 * T)
            layernorm_scalars(dve, 0, SCALE)
            dve.wait_ge(sem("w_loaded"), 16 * 5)

            def body(i):
                j = i + 1
                if j.inside(T):
                    dve.wait_ge(sem2("at_used")[j.slot], j.use)
                    dve.wait_ge(sem2("at_stored")[j.slot], 16 * j.use)
                    for c, (t0, n) in enumerate(HCH):
                        s, use = j.ring(NH, c)
                        dve.wait_ge(sem2("tr_psum")[s], use + 1)
                        nc.vector.tensor_copy(at[j.slot][:, t0:t0 + n, :],
                                              bank16(s)[:, 0:n * P].rearrange("p (t c) -> p t c", c=P))\
                            .then_inc(sem2("at_ready")[j.slot], 1)
                        dve.wait_ge(sem2("at_ready")[j.slot], NH * j.use + c + 1)
                        dve.sem_inc(sem2("tr_free")[s], 1)
                    cols = LAST if (j.static and j.t == T - 1) else P
                    dve.wait_ge(sem("colsum"), j.n + 1)
                    nc.vector.tensor_reduce(cs_tmp[:, :], at[j.slot][:, :, 0:cols], AX.X, ALU.add).then_inc(sem("cs_tmp"), 1)
                    dve.wait_ge(sem("cs_tmp"), j.n + 1)
                    nc.vector.tensor_tensor(colsum[:, :], colsum[:, :], cs_tmp[:, :], ALU.add).then_inc(sem("colsum"), 1)
                if i.inside(T):
                    dve.wait_ge(sem2("agg_lo")[i.slot], i.use + 1)
                    dve.wait_ge(sem2("agg_used")[i.slot], i.use)
                    nc.vector.tensor_tensor(xf_sb[i.slot][:, :], bank[2 + i.slot][:, 0:D], t256[i.slot][:, 0, :], ALU.add)\
                        .then_inc(sem2("agg_sum")[i.slot], 1)
                k = i + -1
                if k.inside(T):
                    dve.wait_ge(sem("hw_psum"), k.n + 1)
                    nc.vector.scalar_tensor_tensor(out=xa[:, k.t, :], in0=b_bc, scalar=rowsum[:, k.t, :],
                                                   in1=bank[5][:, 0:D], op0=ALU.mult, op1=ALU.add).then_inc(sem("hw_done"), 1)
            adj_sweep(dve, body)
            _ = ch

        @block.tensor
        def _(pe):
            pe.wait_ge(sem("w_loaded"), 16 * 5)
            pe.wait_ge(sem("consts"), 2)
            pe.wait_ge(sem("const_chain"), 3)
            for k in range(KD):
                last = nc.tensor.transpose(bank[4][0:DA, k * P:(k + 1) * P], w1_sb[:, k, :], ident[:, :])
            last.then_inc(sem("w1t_psum"), 1)
            pe.wait_ge(sem("w1t"), 1)
            for k in range(KD):
                last = nc.tensor.matmul(bank[5][:, k * DA:(k + 1) * DA], w1t_sb[:, k, :], w2_sb, start=True, stop=True)
            last.then_inc(sem("wq_psum"), 1)
            pe.wait_ge(sem("wq"), 1)
            for u in range(2):
                pe.wait_ge(sem2("norm_lo")[u], T // 2)

            def body(i):
                j, k = i + 1, i + -1
                if j.inside(T):
                    pe.wait_ge(sem2("adj16_ready")[j.slot], j.use + 1)
                    for c, (t0, n) in enumerate(HCH):
                        s, use = j.ring(NH, c)
                        pe.wait_ge(sem2("tr_free")[s], use)
                        for t in range(n):
                            last = nc.tensor.transpose(bank16(s)[:, t * P:(t + 1) * P],
                                                       adj16[j.slot][:, (t0 + t) * P:(t0 + t + 1) * P], ident16[:, :])
                        last.then_inc(sem2("tr_psum")[s], 1)
                        if c == NH - 1:
                            pe.wait_ge(sem2("tr_psum")[s], use + 1)
                            pe.sem_inc(sem2("adj16_free")[j.slot], 1)
                if k.inside(T):
                    pe.wait_ge(sem2("agg_sum")[k.slot], k.use + 1)
                    for c in range(KD):
                        last = nc.tensor.transpose(bank[4][:, c * P:(c + 1) * P], xf_sb[k.slot][:, c * P:(c + 1) * P], ident[:, :])
                    last.then_inc(sem("aggT_psum"), 1)
                if i.inside(T):
                    pe.wait_ge(sem2("at_ready")[i.slot], NH * (i.use + 1))
                    pe.wait_ge(sem2("agg_sum")[i.slot], i.use)
                    for t in range(T):
                        last = nc.tensor.matmul(bank[2 + i.slot][:, :], at[i.slot][:, t, :], parts[:, t, :],
                                                start=(t == 0), stop=(t == T - 1))
                    last.then_inc(sem2("agg_psum")[i.slot], 1)
                    pe.wait_ge(sem2("agg_psum")[i.slot], i.use + 1)
                    pe.sem_inc(sem2("at_used")[i.slot], 1)
                if k.inside(T):
                    pe.wait_ge(sem("aggT"), k.n + 1)
                    pe.sem_inc(sem2("agg_used")[k.slot], 1)
                    pe.wait_ge(sem("hw_done"), k.n)
                    for c in range(KD):
                        last = nc.tensor.matmul(bank[5][:, 0:D], zt[:, c, :], w_sb[:, c, :], start=(c == 0), stop=(c == KD - 1))
                    last.then_inc(sem("hw_psum"), 1)
            adj_sweep(pe, body)

    with nc.Block() as block:

        @block.sync
        def _(sp):
            sp.wait_ge(sem("x1"), T)
            sp.dma_start(x1_d, x_all[:, :, :].rearrange("p t d -> p (t d)")).then_inc(sem("x1_stored"), 16)
            for n, u in enumerate((U1, U2, U3)):
                sp.dma_start(u_sb[:, n, :, :], u[0].rearrange("(k p) n -> p k n", p=P)).then_inc(sem("u_loaded"), 16)

            def body(i):
                sp.wait_ge(sem2("q_out")[i.slot], i.use + 1)
                sp.dma_start(q_d[0, dyn(i)], qs[i.slot][0:DA, :]).then_inc(sem2("q_stored")[i.slot], 16)
            sweep(sp, 0, 2, T // 2 - 1, T, body)
            for u in range(2):
                sp.wait_ge(sem2("q_stored")[u], 16 * (T // 2))
            sp.wait_ge(sem("x1_stored"), 16)
            sp.wait_ge(sem("u_loaded"), 48)

        @block.vector
        def _(dve):
            ch = Chain(dve, "mid_chain")
            ch.link(nc.vector.tensor_tensor(colsum[:, T - 1:T], colsum[:, T - 1:T], padone[:, :], ALU.add))
            ch.link(nc.vector.reciprocal(rdeg[:, :, 0], colsum[:, :]))
            ch.link(nc.vector.tensor_scalar(lt[:, :], colsum[:, :], 1.0, 1e-12, ALU.add, ALU.max))
            ch.link(nc.vector.reciprocal(cinv[:, :, 0], lt[:, :]))
            ch.link(nc.vector.tensor_scalar(lt[:, :], rowsum[:, :, 0], 1.0, 1e-12, ALU.add, ALU.max))
            ch.link(nc.vector.reciprocal(rinv[:, :, 0], lt[:, :]))
            ch.link(nc.vector.tensor_tensor(lt[:, :], lt[:, :], cinv[:, :, 0], ALU.mult))
            ch.link(nc.vector.tensor_reduce(ratio[:, :], lt[:, :], AX.X, ALU.max))
            nc.vector.tensor_scalar(ratio[:, :], ratio[:, :], 1.0, None, ALU.max).then_inc(sem("ratio"), 1)
            dve.wait_ge(sem("ratio_all"), 1)
            ch.link(nc.vector.reciprocal(kappa[:, :], ratio_all[:, :]))
            ch.link(nc.vector.tensor_scalar(rinv_s[:, :, 0], rinv[:, :, 0], 1.0 / SCALE, None, ALU.mult))
            ch.link(nc.vector.tensor_scalar(cinv_r[:, :, 0], cinv[:, :, 0], ratio_all[:, :], 1.0 / SCALE, ALU.mult, ALU.mult))
            def residual(t):
                nc.vector.scalar_tensor_tensor(out=x_all[:, t, :], in0=xa[:, t, :], scalar=rdeg[:, t, :],
                                               in1=x_all[:, t, :], op0=ALU.mult, op1=ALU.add).then_inc(sem("x1"), 1)
            with dve.Fori(0, T // 4) as g:
                for u in range(4):
                    residual(4 * g + u)
            for t in range(T // 4 * 4, T):
                residual(t)
            dve.wait_ge(sem("x1"), T)
            with dve.Fori(0, T // 4) as g:
                for u in range(4):
                    nc.vector.bn_stats(stats[:, 4 * g + u, :], x_all[:, 4 * g + u, :]).then_inc(sem("ln_stats"), 1)
            for t in range(T // 4 * 4, T):
                nc.vector.bn_stats(stats[:, t, :], x_all[:, t, :]).then_inc(sem("ln_stats"), 1)
            dve.wait_ge(sem("ln_stats"), 2 * T)
            for t in range(T):
                nc.vector.bn_aggr(mv[:, t, :], stats[:, t, :]).then_inc(sem("ln_mv"), 1)
            dve.wait_ge(sem("ln_mv"), 2 * T)
            layernorm_scalars(dve, 1, 1.0)

            def body(i):
                dve.wait_ge(sem2("norm_hi")[i.slot], i.use + 1 + T // 2)
                nc.vector.scalar_tensor_tensor(out=parts[:, i.t, D:2 * D], in0=xo_sb[i.slot][:, :], scalar=SCALE,
                                               in1=parts[:, i.t, 0:D], op0=ALU.mult, op1=ALU.subtract)\
                    .then_inc(sem2("norm_lo")[i.slot], 1)
                dve.wait_ge(sem2("qk_psum")[i.slot], i.use + 1)
                dve.wait_ge(sem2("q_stored")[i.slot], 16 * i.use)
                nc.vector.tensor_copy(qs[i.slot][0:DA, :], bank[2 + i.slot][0:DA, 0:P]).then_inc(sem2("q_out")[i.slot], 1)
                nc.vector.tensor_copy(keys[0:DA, bass.ds(i.t * P, P)], bank[2 + i.slot][0:DA, P:2 * P])\
                    .then_inc(sem2("qk_done")[i.slot], 1)
            sweep(dve, 0, 2, T // 2 - 1, T, body)

        @block.gpsimd
        def _(pool):
            pool.wait_ge(sem("ratio"), 1)
            nc.gpsimd.partition_all_reduce(ratio_all[:, :], ratio[:, :], P, bass.bass_isa.ReduceOp.max).then_inc(sem("ratio_all"), 1)

            def body(i):
                pool.wait_ge(sem2("normed")[i.slot], i.use + 1 + T // 2)
                nc.gpsimd.tensor_copy(xa[:, i.t, :], xo_sb[i.slot][:, :]).then_inc(sem2("xa_copied")[i.slot], 1)
            sweep(pool, 0, 2, T // 2 - 1, T, body)

        @block.scalar
        def _(act):
            layernorm_sqrt(act, 1)
            act.wait_ge(sem("ln_ready"), 2)

            def body(i):
                act.wait_ge(sem2("xa_copied")[i.slot], i.use)
                act.wait_ge(sem2("norm_lo")[i.slot], i.use + T // 2)
                act.wait_ge(sem2("XT_psum")[i.slot], i.use)
                nc.scalar.activation(xo_sb[i.slot][:, :], x_all[:, i.t, :], ACT.Relu, bias=lb[:, i.t, :], scale=ly[:, i.t, :])\
                    .then_inc(sem2("normed")[i.slot], 1)
                act.wait_ge(sem2("normed")[i.slot], i.use + 1 + T // 2)
                nc.scalar.activation(parts[:, i.t, 0:D], xo_sb[i.slot][:, :], ACT.Copy, scale=SCALE).then_inc(sem2("norm_hi")[i.slot], 1)
                act.wait_ge(sem2("XT_psum")[i.slot], i.use + 1)
                act.wait_ge(sem2("qk_psum")[i.slot], i.use)
                nc.scalar.activation(t256[i.slot][:, 0, :], bank[i.slot][:, 0:D], ACT.Copy).then_inc(sem2("XT")[i.slot], 1)
            sweep(act, 0, 2, T // 2 - 1, T, body)

        @block.tensor
        def _(pe):
            def body(i):
                pe.wait_ge(sem2("normed")[i.slot], i.use + 1 + T // 2)
                pe.wait_ge(sem2("XT")[i.slot], i.use)
                for c in range(KD):
                    last = nc.tensor.transpose(bank[i.slot][:, c * P:(c + 1) * P], xo_sb[i.slot][:, c * P:(c + 1) * P], ident[:, :])
                last.then_inc(sem2("XT_psum")[i.slot], 1)
                pe.wait_ge(sem2("XT")[i.slot], i.use + 1)
                pe.wait_ge(sem2("qk_done")[i.slot], i.use)
                for n, w in enumerate((wq_sb, w3_sb)):
                    for c in range(KD):
                        last = nc.tensor.matmul(bank[2 + i.slot][0:DA, n * P:(n + 1) * P], w[:, c, :],
                                                t256[i.slot][:, 0, c * P:(c + 1) * P], start=(c == 0), stop=(c == KD - 1))
                last.then_inc(sem2("qk_psum")[i.slot], 1)
            sweep(pe, 0, 2, T // 2 - 1, T, body)

    def diffusion_step(s):
        first = s == 0
        row = slice(s * DA, (s + 1) * DA)
        AB = ACT_BISECTIONS[s]
        AFTER_CHUNK = ((), (0,), (1,), tuple(range(2, 2 * AB - 1)))

        def S(name):
            return sem(f"step_{name}")

        def S2(name):
            return sem2(f"step_{name}")

        def step_sweep(eng, body):
            loops = (T - 6 if eng is nc.sync else T - 4) // 2
            sweep(eng, -1, 3, loops, T + (2 if eng is nc.vector else 1), body, base=s * T)

        with nc.Block() as block:

            @block.sync
            def _(sp):
                def body(i):
                    j, k = i + 1, i + -1
                    if j.inside(T):
                        sp.wait_ge(S2("at_used")[j.slot], j.use)
                        sp.dma_start(at[j.slot][:, :, :].rearrange("p t c -> p (t c)"), adjT_d[dyn(j)])\
                            .then_inc(S2("at_loaded")[j.slot], 16)
                    for ahead in ((1, 2) if i.static and i.t == -1 else (2,)):
                        m = i + ahead
                        if m.inside(T):
                            sp.wait_ge(S2("logits_done")[m.slot], NL * m.use)
                            sp.dma_start(qs[m.slot][row, :], q_d[s, dyn(m)]).then_inc(S2("q_loaded")[m.slot], 16)
                    if not first and i.static and i.t == -1:
                        for n, u in enumerate((U1, U2, U3)):
                            sp.dma_start(u_sb[:, n, :, :], u[s].rearrange("(k p) n -> p k n", p=P)).then_inc(S("u_loaded"), 16)
                        for h in range(2):
                            hs = slice(h * T // 2, (h + 1) * T // 2)
                            sp.dma_start(parts_fb[:, hs, :], fb_d[hs].rearrange("t p c -> p t c")).then_inc(S("fb_loaded"), 16)
                        sp.dma_start(xa[:, :, :], xa_d.rearrange("t p d -> p t d")).then_inc(S("xa_loaded"), 16)
                    if not first and i.inside(T):
                        sp.wait_ge(S2("y_stored")[i.slot], 16 * i.use)
                        sp.dma_start(y_sb[i.slot][:, :], y_d[dyn(i)]).then_inc(S2("y_loaded")[i.slot], 16)
                    if first and k.inside(T):
                        sp.wait_ge(S("qk_done"), k.n + 1)
                        sp.dma_start(q_d[1, dyn(k)], qo[:, :]).then_inc(S("qo_stored"), 16)
                        sp.wait_ge(S2("xo")[k.slot], k.use + 1)
                        sp.dma_start(xa_d[dyn(k)], xo_sb[k.slot][:, :]).then_inc(S2("xo_stored")[k.slot], 16)
                        sp.wait_ge(S2("fb_lo")[k.slot], 2 * (k.use + 1))
                        sp.dma_start(fb_d[dyn(k)], fb_sb[:, :]).then_inc(S2("fb_stored")[k.slot], 16)
                    if k.inside(T):
                        sp.wait_ge(S2("y_done")[k.slot], k.use + 1)
                        sp.dma_start(y_d[dyn(k)], y_sb[k.slot][:, :]).then_inc(S2("y_stored")[k.slot], 16)
                step_sweep(sp, body)
                if first:
                    sp.wait_ge(S("qo_stored"), 16 * T)
                    for u in range(2):
                        sp.wait_ge(S2("xo_stored")[u], 16 * (T // 2))
                        sp.wait_ge(S2("fb_stored")[u], 16 * (T // 2))
                for u in range(2):
                    sp.wait_ge(S2("y_stored")[u], 16 * (s + 1) * (T // 2))

            @block.gpsimd
            def _(pool):
                if first:
                    nc.gpsimd.memset(kept_p[:, N:NP], 0.0).then_inc(S("p_pad"), 1)

                def body(i):
                    j, k = i + 1, i + -1
                    if j.inside(T):
                        pool.wait_ge(S2("at_loaded")[j.slot], 16 * (j.use + 1))
                        nc.gpsimd.tensor_tensor(at[j.slot][:, j.t, :], at[j.slot][:, j.t, :], ident16[:, :], ALU.add)\
                            .then_inc(S2("st_ready")[j.slot], 1)
                    if i.inside(T):
                        for n in range(LOOKS):
                            pool.wait_ge(S("unsettled"), LOOKS * i.n + n + 1)
                            nc.gpsimd.tensor_tensor(pool_tick[:, n:n + 1], padone[:, :], padone[:, :], ALU.add)
                            nc.gpsimd.partition_all_reduce(any_un[:, n:n + 1], unsettled[:, :], P, bass.bass_isa.ReduceOp.max)\
                                .then_inc(S("any_un"), 1)
                    if first and k.inside(T):
                        pool.wait_ge(S2("fb_hi")[k.slot], 3 * (k.use + 1))
                        nc.gpsimd.tensor_tensor(fb_sb[:, D:2 * D], xf_sb[k.slot][:, :], fb_sb[:, 0:D], ALU.subtract)\
                            .then_inc(S2("fb_lo")[k.slot], 1)
                        nc.gpsimd.tensor_tensor(fb_sb[:, 3 * D:4 * D], xk_sb[:, :], fb_sb[:, 2 * D:3 * D], ALU.subtract)\
                            .then_inc(S2("fb_lo")[k.slot], 1)
                step_sweep(pool, body)

            @block.scalar
            def _(act):
                act.wait_ge(S("search_consts"), 1)

                def bisect(j, n):
                    p, o, u = pb[j.slot][:, 0:N], over[j.slot], j.slot
                    ch = Chain(act, "step_bisect", base=ACT_LINKS[s] * j.t + ACT_LINKS[0] * T * s)
                    e = (n - 1) // 2
                    if n == 0:
                        act.wait_ge(S2("negmax")[u], j.use + 1)
                        ch.link(nc.scalar.activation(p, p, ACT.Exp, bias=negmax[u][:, :], accum_out=mass[u][:, 0:1]))
                        ch.link(nc.scalar.activation(o[:, 4:5], mass[u][:, 0:1], ACT.Copy, scale=-NUCLEUS))
                        return
                    ch.count = 2 + 9 * e + (n - 1) % 2
                    if n % 2 == 1:
                        ch.link(nc.scalar.activation(junk_a[:, 0:N], p, ACT.Relu, bias=minus_t[u][:, e:e + 1], accum_out=o[:, 0:1]))
                        return
                    ch.link(nc.scalar.activation(junk_a[:, 0:N], p, ACT.Sign, bias=minus_t[u][:, e:e + 1], accum_out=o[:, 1:2]))
                    m = mass[u][:, 2 + e:3 + e]
                    ch.link(nc.scalar.activation(o[:, 2:3], o[:, 1:2], ACT.Identity, scale=thr[u][:, 2 + e:3 + e], bias=n_t[u][:, e:e + 1]))
                    ch.link(nc.scalar.activation(m, o[:, 2:3], ACT.Identity, scale=0.5, bias=o[:, 0:1]))
                    ch.link(nc.scalar.activation(o[:, 3:4], m, ACT.Sign, bias=o[:, 4:5]))
                    ch.link(nc.scalar.activation(log_t[u][:, e + 1:e + 2], o[:, 3:4], ACT.Identity, scale=RANGE / 2 ** (e + 2),
                                                 bias=log_t[u][:, e:e + 1]))
                    nt = thr[u][:, 3 + e:4 + e]
                    ch.link(nc.scalar.activation(nt, log_t[u][:, e + 1:e + 2], ACT.Exp))
                    if e + 1 < AB:
                        ch.link(nc.scalar.activation(minus_t[u][:, e + 1:e + 2], nt, ACT.Copy, scale=-1.0))
                        ch.link(nc.scalar.activation(n_t[u][:, e + 1:e + 2], nt, ACT.Copy, scale=float(N)))
                    else:
                        assert ch.count == ACT_LINKS[s], ch.count
                        act.sem_inc(S2("p_ready")[u], 1)

                def body(i):
                    j, k = i + 1, i + -1
                    if j.inside(T):
                        act.wait_ge(S2("masked")[j.slot], j.use)
                        for c, (c0, w) in enumerate(LCH):
                            sl, use = j.ring(NL, c)
                            act.wait_ge(S2("logits_psum")[sl], use + 1)
                            nc.scalar.activation(pb[j.slot][:, c0:c0 + w], bank[sl][:, 0:w], ACT.Copy).then_inc(S2("logits_done")[j.slot], 1)
                            act.wait_ge(S2("logits_done")[j.slot], NL * j.use + c + 1)
                            act.sem_inc(S2("logits_free")[sl], 1)
                    for c, (t0, n) in enumerate(TCH):
                        if k.inside(T):
                            sl, use = k.ring(NT, c)
                            act.wait_ge(S2("pt_psum")[sl], use + 1)
                            act.wait_ge(S2("pt_used")[sl], use)
                            nc.scalar.activation(pt[sl][:, 0:n * P], pt_ps[sl][:, 0:n * P], ACT.Copy).then_inc(S2("pt")[sl], 1)
                        if j.inside(T):
                            for n in AFTER_CHUNK[c]:
                                bisect(j, n)
                    if k.inside(T):
                        act.wait_ge(S("px_psum"), k.n + 1)
                        act.wait_ge(S2("xoT_psum_of")[k.slot], k.use)
                        if first:
                            act.wait_ge(S2("xo_stored")[k.slot], 16 * k.use)
                        nc.scalar.activation(xo_sb[k.slot][:, :], bank[4][:, 0:D], ACT.Copy, scale=rkept[k.slot][:, :])\
                            .then_inc(S2("xo")[k.slot], 1)
                        act.wait_ge(S("fbT_psum"), k.n + 1)
                        act.wait_ge(S("z_psum"), k.n)
                        nc.scalar.activation(zt[:, 0:4, :].rearrange("p k c -> p (k c)"), bank[7][:, :], ACT.Copy,
                                             scale=(1.0 / SCALE if first else 1.0)).then_inc(S("fbT"), 1)
                    if j.inside(T):
                        bisect(j, 2 * AB - 1)
                    if i.inside(T):
                        act.wait_ge(S("sx_psum"), i.n + 1)
                        if first:
                            for n, sc in enumerate((rinv, cinv)):
                                nc.scalar.activation(t256[i.slot][:, n, :], bank[5][:, D:2 * D], ACT.Copy, scale=sc[:, i.t, :])\
                                    .then_inc(S2("sx_lo")[i.slot], 1)
                        else:
                            for n, sc in enumerate((rinv_s, cinv_r)):
                                nc.scalar.activation(t256[i.slot][:, n, :], bank[5 + n][:, D:2 * D], ACT.Copy, scale=sc[:, i.t, :])\
                                    .then_inc(S2("sx_lo")[i.slot], 1)
                    if k.inside(T):
                        act.wait_ge(S("xoT_psum"), k.n + 1)
                        nc.scalar.activation(zt[:, 4:6, :].rearrange("p k c -> p (k c)"), bank[7][:, 0:D], ACT.Copy).then_inc(S("xoT"), 1)
                    if j.inside(T):
                        bisect(j, 2 * AB)
                    if first and k.inside(T):
                        fb = fb_sb
                        act.wait_ge(S2("xfb")[k.slot], 2 * (k.use + 1))
                        act.wait_ge(S2("fb_stored")[1 - k.slot], 16 * (k + 1).use)
                        nc.scalar.activation(fb[:, 0:D], xf_sb[k.slot][:, :], ACT.Copy).then_inc(S2("fb_hi")[k.slot], 1)
                        act.wait_ge(S2("fb_lo")[1 - k.slot], 2 * (k + 1).use)
                        nc.scalar.activation(xk_sb[:, :], xb_sb[k.slot][:, :], ACT.Copy, scale=kappa[:, :]).then_inc(S2("fb_hi")[k.slot], 1)
                        act.wait_ge(S2("fb_hi")[k.slot], 3 * k.use + 2)
                        nc.scalar.activation(fb[:, 2 * D:3 * D], xk_sb[:, :], ACT.Copy).then_inc(S2("fb_hi")[k.slot], 1)
                    if first and k.inside(T):
                        act.wait_ge(S("z_psum"), k.n + 1)
                        r1 = slice(DA, 2 * DA)
                        act.wait_ge(S("qo_stored"), 16 * k.n)
                        nc.scalar.activation(qo[:, :], bank[7][0:DA, D:D + P], ACT.Copy)
                        nc.scalar.activation(keys[r1, bass.ds(k.t * P, P)], bank[7][0:DA, D + P:D + 2 * P], ACT.Copy)\
                            .then_inc(S("qk_done"), 1)
                step_sweep(act, body)

            @block.vector
            def _(dve):
                bisections, interpolations, aim = SEARCH[s]
                K = 2 + bisections
                if first:
                    nc.vector.memset(ones8[:, :], 1.0)
                    for u in range(2):
                        for c, v in ((0, math.exp(-RANGE)), (1, 1.0 + 1e-6), (2, math.exp(-RANGE / 2))):
                            nc.vector.memset(thr[u][:, c:c + 1], v)
                        nc.vector.memset(mass[u][:, 1:2], 0.0)
                        nc.vector.memset(log_t[u][:, 0:1], -RANGE / 2)
                        nc.vector.memset(minus_t[u][:, 0:1], -math.exp(-RANGE / 2))
                        nc.vector.memset(n_t[u][:, 0:1], N * math.exp(-RANGE / 2))
                    nc.vector.tensor_scalar(nucleus_pad[:, :], padone[:, :], 0.5 / N - NUCLEUS, NUCLEUS, ALU.mult, ALU.add)
                    last = nc.vector.memset(below[:, N:N + 8], 0.0)
                    last.then_inc(S("search_consts"), 1)
                    dve.wait_ge(S("search_consts"), 1)

                def evaluate(ch, p, t, m):
                    ch.link(nc.vector.scalar_tensor_tensor(out=junk_v[:, 0:N], in0=p, scalar=t, in1=p,
                                                           op0=ALU.is_ge, op1=ALU.mult, accum_out=m))

                def narrow(ch, p):
                    evaluate(ch, p, cur[:, 0:1], cur[:, 1:2])
                    nc.vector.tensor_scalar(m_lo[:, :], cur[:, 1:2], target[:, :], None, ALU.is_ge)
                    ch.link(nc.vector.tensor_scalar(m_hi[:, :], cur[:, 1:2], target[:, :], None, ALU.is_lt), hold=True)
                    nc.vector.copy_predicated(lo[:, :], m_lo[:, :].to_broadcast([P, 2]), cur[:, :])
                    ch.link(nc.vector.copy_predicated(hi[:, :], m_hi[:, :].to_broadcast([P, 2]), cur[:, :]))

                def search(i):
                    p, th, ms = pb[i.slot][:, 0:N], thr[i.slot], mass[i.slot]
                    ch = Chain(dve, "step_search", base=i.t * LINKS[s] + sum(LINKS[:s]) * T)
                    dve.wait_ge(S2("p_ready")[i.slot], i.use + 1)
                    if i.static and i.t == T - 1:
                        ch.link(nc.vector.tensor_scalar(target[:, :], ms[:, 0:1], nucleus_pad[:, :], None, ALU.mult))
                    else:
                        ch.link(nc.vector.tensor_scalar(target[:, :], ms[:, 0:1], NUCLEUS, None, ALU.mult))
                    for e in range(AB, bisections):
                        evaluate(ch, p, th[:, 2 + e:3 + e], ms[:, 2 + e:3 + e])
                        if e < bisections - 1:
                            d = RANGE / 2 ** (e + 2)
                            up, down = math.exp(d), math.exp(-d)
                            ch.link(nc.vector.tensor_scalar(factor[:, :], ms[:, 2 + e:3 + e], target[:, :], up - down, ALU.is_ge, ALU.mult))
                            ch.link(nc.vector.scalar_tensor_tensor(out=th[:, 3 + e:4 + e], in0=factor[:, :], scalar=down,
                                                                   in1=th[:, 2 + e:3 + e], op0=ALU.add, op1=ALU.mult))
                    t, m, f, w = th[:, 0:K], ms[:, 0:K], is_lo[:, 0:K], wk[:, 0:K]
                    ch.link(nc.vector.tensor_scalar(f, m, target[:, :], None, ALU.is_ge))
                    ch.link(nc.vector.tensor_tensor(w, f, t, ALU.mult))
                    ch.link(nc.vector.tensor_reduce(lo[:, 0:1], w, AX.X, ALU.max))
                    ch.link(nc.vector.scalar_tensor_tensor(out=w, in0=f, scalar=BIG, in1=t, op0=ALU.mult, op1=ALU.add))
                    ch.link(nc.vector.tensor_reduce(hi[:, 0:1], w, AX.X, ALU.min))
                    ch.link(nc.vector.scalar_tensor_tensor(out=w, in0=f, scalar=-BIG, in1=m, op0=ALU.mult, op1=ALU.add))
                    ch.link(nc.vector.tensor_reduce(hi[:, 1:2], w, AX.X, ALU.max))
                    ch.link(nc.vector.tensor_scalar(w, f, -BIG, BIG, ALU.mult, ALU.add))
                    ch.link(nc.vector.tensor_tensor(w, w, m, ALU.add))
                    ch.link(nc.vector.tensor_reduce(lo[:, 1:2], w, AX.X, ALU.min))
                    row_max(i + 1)
                    spread(i + -1)
                    add_z(i + -2)
                    for e in range(interpolations):
                        nc.vector.tensor_tensor(frac[:, 0:1], lo[:, 1:2], hi[:, 1:2], ALU.subtract)
                        ch.link(nc.vector.scalar_tensor_tensor(out=frac[:, 1:2], in0=hi[:, 0:1], scalar=-aim, in1=target[:, :],
                                                               op0=ALU.mult, op1=ALU.add))
                        nc.vector.tensor_scalar(frac[:, 1:2], frac[:, 1:2], hi[:, 1:2], 0.0, ALU.subtract, ALU.max)
                        nc.vector.tensor_tensor(frac[:, 2:3], hi[:, 0:1], lo[:, 0:1], ALU.subtract)
                        ch.link(nc.vector.reciprocal(frac[:, 0:1], frac[:, 0:1]))
                        ch.link(nc.vector.scalar_tensor_tensor(out=frac[:, 3:4], in0=frac[:, 1:2], scalar=frac[:, 0:1], in1=frac[:, 2:3],
                                                               op0=ALU.mult, op1=ALU.mult))
                        ch.link(nc.vector.tensor_tensor(cur[:, 0:1], hi[:, 0:1], frac[:, 3:4], ALU.subtract))
                        narrow(ch, p)
                    ch.link(nc.vector.scalar_tensor_tensor(out=below[:, 0:N], in0=p, scalar=hi[:, 0:1], in1=p,
                                                           op0=ALU.is_lt, op1=ALU.mult, accum_out=below_sum[:, :]))
                    nc.vector.tensor_copy(edges[:, 8:9], hi[:, 0:1])
                    ch.link(nc.vector.tensor_tensor(run9[:, 0:1], ms[:, 0:1], below_sum[:, :], ALU.subtract), hold=True)
                    ch.link(nc.vector.max(top8[:, :], below[:, :]))
                    take(ch)
                    ch.link(nc.vector.tensor_scalar(left[:, :], run9[:, 0:8], target[:, :], BIG, ALU.is_ge, ALU.mult))
                    ch.link(nc.vector.tensor_tensor(edges[:, 0:8], left[:, :], top8[:, :], ALU.max))
                    ch.link(nc.vector.tensor_reduce(edge[:, :], edges[:, :], AX.X, ALU.min))
                    ch.link(nc.vector.tensor_tensor(left[:, :], top8[:, :], take8[:, :], ALU.subtract))
                    ch.link(nc.vector.tensor_reduce(left_max[:, :], left[:, :], AX.X, ALU.max))
                    ch.link(nc.vector.tensor_scalar(tied[:, :], left_max[:, :], edge[:, :], None, ALU.is_ge))
                    dve.wait_ge(S("any_un"), LOOKS * i.n)
                    ch.link(nc.vector.scalar_tensor_tensor(out=unsettled[:, :], in0=left_max[:, :], scalar=0.0, in1=tied[:, :],
                                                           op0=ALU.is_le, op1=ALU.max))
                    dve.sem_inc(S("unsettled"), 1)
                    add_taken(ch)
                    dve.wait_ge(S("p_used"), i.n)
                    ch.link(nc.vector.scalar_tensor_tensor(out=kept_p[:, 0:N], in0=p, scalar=edge[:, :], in1=p,
                                                           op0=ALU.is_ge, op1=ALU.mult, accum_out=edge_mass[:, :]))
                    assert ch.count == LINKS[s], ch.count

                def take(ch):
                    ch.link(nc.vector.tensor_tensor_scan(run9[:, 1:9], ones8[:, :], top8[:, :], run9[:, 0:1], ALU.mult, ALU.add))
                    ch.link(nc.vector.scalar_tensor_tensor(out=take8[:, :], in0=run9[:, 0:8], scalar=target[:, :], in1=top8[:, :],
                                                           op0=ALU.is_lt, op1=ALU.mult, accum_out=took[:, :]))

                def add_taken(ch):
                    ch.link(nc.vector.tensor_tensor(run9[:, 0:1], run9[:, 0:1], took[:, :], ALU.add))

                def remove(ch):
                    ch.link(nc.vector.match_replace(below[:, :], take8[:, :], below[:, :], 0.0), hold=True)

                def is_unsettled(ch):
                    ch.link(nc.vector.tensor_scalar(unsettled[:, :], run9[:, 0:1], target[:, :], None, ALU.is_lt), hold=True)

                def look(i, n):
                    dve.wait_ge(S("any_un"), LOOKS * i.n + n)
                    nc.vector.memset(tick[:, n:n + 1], 0.0)
                    return dve.value_load(any_un[0:1, n - 1:n].bitcast(i32))

                def spread(i):
                    if not i.inside(T):
                        return
                    dve.wait_ge(S2("sx_lo")[i.slot], 2 * (i.use + 1))
                    if first:
                        dve.wait_ge(S2("fb_lo")[i.slot], 2 * i.use)
                    dve.wait_ge(S2("fbT_psum_of")[i.slot], i.use)
                    for n, (dst, sc) in enumerate(((xf_sb, rinv if first else rinv_s), (xb_sb, cinv if first else cinv_r))):
                        nc.vector.scalar_tensor_tensor(out=dst[i.slot][:, :], in0=bank[5 if first else 5 + n][:, 0:D],
                                                       scalar=sc[:, i.t, :], in1=t256[i.slot][:, n, :],
                                                       op0=ALU.mult, op1=ALU.add).then_inc(S2("xfb")[i.slot], 1)

                def add_z(k):
                    if not k.inside(T):
                        return
                    dve.wait_ge(S("z_psum"), k.n + 1)
                    if first:
                        dve.wait_ge(S("qk_done"), k.n + 1)
                        dve.wait_ge(S2("y_stored")[k.slot], 16 * k.use)
                        nc.vector.tensor_tensor(y_sb[k.slot][:, :], bank[7][:, 0:D], xa[:, k.t, :], ALU.add).then_inc(S2("y_done")[k.slot], 1)
                    else:
                        dve.wait_ge(S2("y_loaded")[k.slot], 16 * (k.use_here + 1))
                        nc.vector.tensor_tensor(y_sb[k.slot][:, :], bank[7][:, 0:D], y_sb[k.slot][:, :], ALU.add).then_inc(S("y_sum"), 1)
                        dve.wait_ge(S("y_sum"), k.t + 1)
                        nc.vector.bn_stats(stats[:, k.t, :], y_sb[k.slot][:, :]).then_inc(S2("y_done")[k.slot], 1)

                def row_max(j):
                    if j.inside(T):
                        dve.wait_ge(S2("logits_done")[j.slot], NL * (j.use + 1))
                        nc.vector.tensor_reduce(negmax[j.slot][:, :], pb[j.slot][:, 0:N], AX.X, ALU.max, negate=True)\
                            .then_inc(S2("negmax")[j.slot], 1)

                def a_round(ch):
                    ch.link(nc.vector.max(top8[:, :], below[:, :]))
                    take(ch)
                    add_taken(ch)
                    is_unsettled(ch)
                    remove(ch)

                def ties(ch):
                    q, count = kept_p[:, 0:N], below[:, 0:N]
                    nc.vector.tensor_scalar(tie[:, 0:1], edge[:, :], 1e-30, None, ALU.max)
                    nc.vector.tensor_scalar(tie[:, 1:2], edge[:, :], -1.0, None, ALU.mult)
                    nc.vector.tensor_scalar(unsettled[:, :], edge_mass[:, :], target[:, :], None, ALU.is_lt)
                    ch.link(nc.vector.tensor_scalar(junk_v[:, 0:N], q, edge[:, :], None, ALU.is_equal))
                    nc.vector.reciprocal(tie[:, 0:1], tie[:, 0:1])
                    ch.link(nc.vector.tensor_tensor_scan(count, ones8[:, 0:1].to_broadcast([P, N]), junk_v[:, 0:N], 0.0, ALU.mult, ALU.add))
                    ch.link(nc.vector.scalar_tensor_tensor(out=tie[:, 2:3], in0=below[:, N - 1:N], scalar=edge[:, :], in1=edge_mass[:, :],
                                                           op0=ALU.mult, op1=ALU.subtract))
                    ch.link(nc.vector.tensor_tensor(tie[:, 2:3], tie[:, 2:3], target[:, :], ALU.add))
                    ch.link(nc.vector.tensor_scalar(tie[:, 3:4], tie[:, 2:3], tie[:, 0:1], 1.0, ALU.mult, ALU.add))
                    ch.link(nc.vector.scalar_tensor_tensor(out=count, in0=count, scalar=tie[:, 3:4], in1=junk_v[:, 0:N],
                                                           op0=ALU.is_ge, op1=ALU.mult))
                    ch.link(nc.vector.scalar_tensor_tensor(out=q, in0=count, scalar=tie[:, 1:2], in1=q, op0=ALU.mult, op1=ALU.add,
                                                           accum_out=run9[:, 0:1]), hold=True)

                def settle(i):
                    p, q, d = pb[i.slot][:, 0:N], kept_p[:, 0:N], below[:, 0:N]
                    with dve.If(look(i, 1) > 0):
                        c1 = Chain(dve, "step_settle_1", base=TIES * i.n)
                        ties(c1)
                        assert c1.count == TIES - 1, c1.count
                        dve.sem_inc(S("settle_1"), 1)
                        dve.sem_inc(S("unsettled"), 1)
                        with dve.If(look(i, 2) > 0):
                            c2 = Chain(dve, "step_settle_2", base=FEW * i.n)
                            c2.link(nc.vector.tensor_tensor(d, p, q, ALU.subtract), hold=True)
                            for _ in range(FEW_ROUNDS):
                                a_round(c2)
                            dve.sem_inc(S("unsettled"), 1)
                            with dve.If(look(i, 3) > 0):
                                with dve.Fori(0, ALL_ROUNDS) as g:
                                    a_round(Chain(dve, "step_settle_3", base=TAKE * ALL_ROUNDS * i.n + TAKE * g))
                            with dve.Else():
                                dve.sem_inc(S("settle_3"), TAKE * ALL_ROUNDS)
                            c2.link(nc.vector.tensor_tensor(q, p, d, ALU.subtract), hold=True)
                            assert c2.count == FEW, c2.count
                        with dve.Else():
                            dve.sem_inc(S("settle_2"), FEW)
                            dve.sem_inc(S("settle_3"), TAKE * ALL_ROUNDS)
                            dve.sem_inc(S("unsettled"), 1)
                    with dve.Else():
                        dve.sem_inc(S("settle_1"), TIES)
                        dve.sem_inc(S("settle_2"), FEW)
                        dve.sem_inc(S("settle_3"), TAKE * ALL_ROUNDS)
                        dve.sem_inc(S("unsettled"), 2)

                def body(i):
                    j, k = i + 1, i + -1
                    if i.inside(T):
                        search(i)
                    if i.inside(T):
                        settle(i)
                        dve.wait_ge(S2("xo")[i.slot], i.use)
                        nc.vector.reciprocal(rkept[i.slot][:, :], run9[:, 0:1]).then_inc(S2("masked")[i.slot], 1)
                    if not i.inside(T):
                        row_max(j)
                        spread(k)
                        add_z(k + -1)
                step_sweep(dve, body)

            @block.tensor
            def _(pe):
                def body(i):
                    j, k = i + 1, i + -1
                    if j.inside(T):
                        pe.wait_ge(S2("q_loaded")[j.slot], 16 * (j.use + 1))
                        for c, (c0, w) in enumerate(LCH):
                            sl, use = j.ring(NL, c)
                            pe.wait_ge(S2("logits_free")[sl], use)
                            nc.tensor.matmul(bank[sl][:, 0:w], qs[j.slot][row, :], keys[row, c0:c0 + w], start=True, stop=True)\
                                .then_inc(S2("logits_psum")[sl], 1)
                    if k.inside(T):
                        pe.wait_ge(S2("masked")[k.slot], k.use + 1)
                        pe.wait_ge(S("p_pad"), 1)

                        def transposes(c):
                            t0, n = TCH[c]
                            sl, use = k.ring(NT, c)
                            pe.wait_ge(S2("pt")[sl], use)
                            if pt_ps[sl] is pairs[0] and j.inside(T):
                                for c1 in (NL - 2, NL - 1):
                                    ls, lu = j.ring(NL, c1)
                                    pe.wait_ge(S2("logits_free")[ls], lu + 1)
                            for t in range(n):
                                last = nc.tensor.transpose(pt_ps[sl][:, t * P:(t + 1) * P],
                                                           kept_p[:, (t0 + t) * P:(t0 + t + 1) * P], ident[:, :])
                            last.then_inc(S2("pt_psum")[sl], 1)

                        def product(c):
                            t0, n = TCH[c]
                            sl, use = k.ring(NT, c)
                            pe.wait_ge(S2("pt")[sl], use + 1)
                            for t in range(n):
                                last = nc.tensor.matmul(bank[4][:, 0:D], pt[sl][:, t * P:(t + 1) * P], xa[:, t0 + t, :],
                                                        start=(t0 + t == 0), stop=(t0 + t == T - 1))
                            last.then_inc(S2("pt_used")[sl], 1)

                        if not first and k.static and k.t == 0:
                            pe.wait_ge(S("xa_loaded"), 16)
                            pe.wait_ge(S("u_loaded"), 48)
                        transposes(0)
                        pe.wait_ge(S2("xo")[1 - k.slot], (k + 1).use)
                        for c in range(NT):
                            if c + 1 < NT:
                                transposes(c + 1)
                            product(c)
                        sl, use = k.ring(NT, NT - 1)
                        pe.wait_ge(S2("pt_used")[sl], use + 1)
                        pe.sem_inc(S("p_used"), 1)
                        pe.sem_inc(S("px_psum"), 1)
                        pe.wait_ge(S2("xfb")[k.slot], 2 * (k.use + 1))
                        pe.wait_ge(S2("y_done")[1 - k.slot], (k + 1).use)
                        if first:
                            pe.wait_ge(S("qk_done"), k.n)
                        for n, src in enumerate((xf_sb, xb_sb)):
                            for c in range(KD):
                                q = n * KD + c
                                last = nc.tensor.transpose(bank[7][:, q * P:(q + 1) * P], src[k.slot][:, c * P:(c + 1) * P], ident[:, :])
                        last.then_inc(S("fbT_psum"), 1)
                        pe.wait_ge(S("fbT_psum"), k.n + 1)
                        pe.sem_inc(S2("fbT_psum_of")[k.slot], 1)
                    if i.inside(T):
                        if not first:
                            pe.wait_ge(S("fb_loaded"), 32)
                        pe.wait_ge(S2("st_ready")[i.slot], i.use + 1)
                        pe.wait_ge(S2("xfb")[1 - i.slot], 2 * (i + 1).use)
                        for n in range(1 if first else 2):
                            for t in range(T):
                                mov = parts[:, t, :] if first else parts_fb[:, t, n * 2 * D:(n + 1) * 2 * D]
                                last = nc.tensor.matmul(bank[5 + n][:, :], at[i.slot][:, t, :], mov, start=(t == 0), stop=(t == T - 1))
                        last.then_inc(S("sx_psum"), 1)
                        pe.wait_ge(S("sx_psum"), i.n + 1)
                        pe.sem_inc(S2("at_used")[i.slot], 1)
                    if k.inside(T):
                        pe.wait_ge(S2("xo")[k.slot], k.use + 1)
                        pe.wait_ge(S("fbT"), k.n + 1)
                        for c in range(KD):
                            last = nc.tensor.transpose(bank[7][:, c * P:(c + 1) * P], xo_sb[k.slot][:, c * P:(c + 1) * P], ident[:, :])
                        last.then_inc(S("xoT_psum"), 1)
                        pe.wait_ge(S("xoT_psum"), k.n + 1)
                        pe.sem_inc(S2("xoT_psum_of")[k.slot], 1)
                    if k.inside(T):
                        pe.wait_ge(S("xoT"), k.n + 1)
                        for q in range(6):
                            last = nc.tensor.matmul(bank[7][:, 0:D], zt[:, q, :], u_sb[:, q // KD, q % KD, :],
                                                    start=(q == 0), stop=(q == 5))
                        if first:
                            for n, w in enumerate((wq_sb, w3_sb)):
                                for c in range(KD):
                                    last = nc.tensor.matmul(bank[7][0:DA, D + n * P:D + (n + 1) * P], w[:, c, :], zt[:, 4 + c, :],
                                                            start=(c == 0), stop=(c == KD - 1))
                        last.then_inc(S("z_psum"), 1)
                step_sweep(pe, body)

    diffusion_step(0)
    diffusion_step(1)

    H = T // 4 * 2
    OUT_PARTS = ((0, H), (H, T))
    with nc.Block() as block:

        @block.sync
        def _(sp):
            sp.dma_start(gamma_bc, bc(gamma)).then_inc(sem2("out_in")[0], 16)
            sp.dma_start(beta_bc, bc(beta)).then_inc(sem2("out_in")[0], 16)
            for h, (t0, t1) in enumerate(OUT_PARTS):
                sp.dma_start(yall[:, t0:t1, :], y_d[t0:t1].rearrange("t p d -> p t d")).then_inc(sem2("out_in")[h], 16)
                sp.dma_start(xa[:, t0:t1, :].rearrange("p t d -> p (t d)"), x1_d[:, t0 * D:t1 * D]).then_inc(sem2("out_in")[h], 16)

            def body(i):
                sp.wait_ge(sem2("o_done")[i.slot], i.use + 1)
                sp.dma_start(out_t[dyn(i)], xo_sb[i.slot][:, :]).then_inc(sem2("o_stored")[i.slot], 16)
            out_t = out[0:(T - 1) * P, :].rearrange("(t p) n -> t p n", p=P)
            sweep(sp, 0, 2, (T - 1) // 2 - 1, T - 1, body)
            i = Idx(0, T - 1)
            sp.wait_ge(sem2("o_done")[i.slot], i.use + 1)
            even = LAST - LAST % 16
            for r0, r1 in ((0, even), (even, LAST)):
                if r1 > r0:
                    sp.dma_start(out[(T - 1) * P + r0:(T - 1) * P + r1, :], xo_sb[i.slot][r0:r1, :]).then_inc(sem("o_last_stored"), 16)
            sp.wait_ge(sem("o_last_stored"), 16 * (2 if LAST % 16 and LAST > 16 else 1))
            sp.wait_ge(sem2("o_stored")[0], 16 * (T // 2))
            sp.wait_ge(sem2("o_stored")[1], 16 * (T // 2 - 1))

        @block.scalar
        def _(act):
            layernorm_sqrt(act, 2)
            act.wait_ge(sem("ln_ready"), 3)

            def body(i):
                act.wait_ge(sem2("o_done")[i.slot], i.use)
                nc.scalar.activation(xf_sb[i.slot][:, :], yall[:, i.t, :], ACT.Identity, bias=lb[:, i.t, :], scale=ly[:, i.t, :])\
                    .then_inc(sem2("normed")[i.slot], 1)
            for h, (t0, t1) in enumerate(OUT_PARTS):
                act.wait_ge(sem2("out_in")[h], 64 if h == 0 else 32)
                sweep(act, t0, t0 + 2, (t1 - t0) // 2 - 1, t1, body)

        @block.vector
        def _(dve):
            for u in range(2):
                dve.wait_ge(sem2("step_y_done")[u], T)
            for t in range(T):
                nc.vector.bn_aggr(mv[:, t, :], stats[:, t, :]).then_inc(sem("ln_mv"), 1)
            dve.wait_ge(sem("ln_mv"), 3 * T)
            layernorm_scalars(dve, 2, 1.0)

            def body(i):
                ch = Chain(dve, "ln_chain", base=21 + 2 * i.n)
                dve.wait_ge(sem2("normed")[i.slot], i.use + 1 + T)
                ch.link(nc.vector.tensor_tensor(xb_sb[i.slot][:, :], xf_sb[i.slot][:, :], gamma_bc, ALU.mult))
                ch.link(nc.vector.tensor_tensor(xb_sb[i.slot][:, :], xb_sb[i.slot][:, :], beta_bc, ALU.add))
                dve.wait_ge(sem2("o_stored")[i.slot], 16 * i.use)
                nc.vector.tensor_tensor(xo_sb[i.slot][:, :], xb_sb[i.slot][:, :], xa[:, i.t, :], ALU.add).then_inc(sem2("o_done")[i.slot], 1)
            for h, (t0, t1) in enumerate(OUT_PARTS):
                dve.wait_ge(sem2("out_in")[h], 64 if h == 0 else 32)
                sweep(dve, t0, t0 + 2, (t1 - t0) // 2 - 1, t1, body)


_INS = ["x", "adj", "L0_gnn_W", "L0_gnn_b", "L1_gnn_W1", "L1_gnn_W2", "L1_gnn_W3",
        "L1_gnn_U1", "L1_gnn_U2", "L1_gnn_U3", "L1_gnn_gamma", "L1_gnn_beta"]


def kernel(**inputs):
    import numpy as _np
    import concourse.bacc as _bacc
    from concourse import mybir as _mybir
    from concourse.bass_utils import run_bass_kernel_spmd as _run

    nc = _bacc.Bacc("TRN2", target_bir_lowering=False, num_devices=1)
    arrays, args = {}, []
    for name in _INS:
        a = _np.ascontiguousarray(inputs[name])
        arrays[f"in_{name}_dram"] = a
        args.append(nc.dram_tensor(f"in_{name}_dram", a.shape, _mybir.dt.from_np(a.dtype), kind="ExternalInput").ap())
    o = nc.dram_tensor("out_0_dram", inputs["x"].shape, _mybir.dt.float32, kind="ExternalOutput").ap()
    gnn_program(nc, *args, o)
    r = _run(nc, [arrays], core_ids=[0])
    return r.results[0]["out_0_dram"]
```
